# Optimizing a Trainium2 kernel written in Bass

```python
import numpy as np
import jax
import jax.numpy as jnp

def _softmax(x, axis=-1):
    return jax.nn.softmax(x, axis=axis)

def _gelu(x):
    return jax.nn.gelu(x, approximate=True)

def _silu(x):
    return jax.nn.silu(x)

def _sigmoid(x):
    return jax.nn.sigmoid(x)

def _layernorm(x, axis=-1, eps=1e-05):
    m = jnp.mean(x, axis=axis, keepdims=True)
    v = jnp.var(x, axis=axis, keepdims=True)
    return (x - m) / jnp.sqrt(v + eps)

def _scatter_add(tgt, idx, src, axis=0):
    return tgt.at[idx].add(src)

def _segment_sum(src, seg, n):
    return jax.ops.segment_sum(src, seg, n)
kernel_name = 'mk_gnn_preln_d2_gnn_r32_004d2e'

def setup_inputs(seed: int=0):
    np.random.seed(seed)
    _w = jnp.asarray

    def _rec_inputs():
        import jax
        import jax.numpy as jnp
        _gk = jax.random.key(seed)
        x = -0.000202 + 1 * jax.random.normal(jax.random.fold_in(_gk, 1), (3125, 64), jnp.float32)
        _s = jax.random.randint(jax.random.fold_in(_gk, 2), (25000,), 0, 3125, jnp.int32)
        _d = jax.random.randint(jax.random.fold_in(_gk, 3), (25000,), 0, 3125, jnp.int32)
        _loop = jnp.arange(3125, dtype=jnp.int32)
        src = jnp.concatenate([_s, _d, _loop])
        dst = jnp.concatenate([_d, _s, _loop])
        _o = jnp.argsort(dst, stable=True)
        src = src[_o]
        dst = dst[_o]
        edge_attr_32 = 0.000196303 + 1.00016 * jax.random.normal(jax.random.fold_in(_gk, 11), (53125, 32), jnp.float32)
        return (x, src, dst, edge_attr_32)
    x, src, dst, edge_attr_32 = _rec_inputs()

    def _L0_gnn_setup():
        import jax, jax.numpy as jnp
        import numpy as np
        N = 3125
        E = 50000
        DIM = 64
        H = 4
        HD = DIM // H
        FF = 4 * DIM

        def _layernorm(x, g, b, eps=1e-05):
            m = x.mean(-1, keepdims=True)
            v = ((x - m) ** 2).mean(-1, keepdims=True)
            return (x - m) / jnp.sqrt(v + eps) * g + b
        key = jax.random.key(seed)
        ks = jax.random.split(key, 12)
        s = 1.0 / np.sqrt(DIM)
        return {'x': jax.random.normal(ks[0], (N, DIM), jnp.float32), 'edge_index': jax.random.randint(ks[1], (2, E), 0, N, jnp.int32), 'w_q': jax.random.normal(ks[2], (DIM, DIM), jnp.float32) * s, 'w_k': jax.random.normal(ks[3], (DIM, DIM), jnp.float32) * s, 'w_v': jax.random.normal(ks[4], (DIM, DIM), jnp.float32) * s, 'w_o': jax.random.normal(ks[5], (DIM, DIM), jnp.float32) * s, 'ln1_g': jnp.ones((DIM,), jnp.float32), 'ln1_b': jnp.zeros((DIM,), jnp.float32), 'ln2_g': jnp.ones((DIM,), jnp.float32), 'ln2_b': jnp.zeros((DIM,), jnp.float32), 'ff1_w': jax.random.normal(ks[6], (DIM, FF), jnp.float32) * s, 'ff1_b': jnp.zeros((FF,), jnp.float32), 'ff2_w': jax.random.normal(ks[7], (FF, DIM), jnp.float32) * (1.0 / np.sqrt(FF)), 'ff2_b': jnp.zeros((DIM,), jnp.float32)}
    _L0_gnn_all = _L0_gnn_setup()
    _L0_gnn_in = {k: v for k, v in _L0_gnn_all.items() if k in ('w_q', 'w_k', 'w_v', 'w_o', 'ln1_g', 'ln1_b', 'ln2_g', 'ln2_b', 'ff1_w', 'ff1_b', 'ff2_w', 'ff2_b')}
    del _L0_gnn_all

    def _L1_gnn_setup():
        import jax, jax.numpy as jnp
        import numpy as np
        N_NODES = 50000
        N_EDGES = 25000
        IN_CH = 64
        OUT_CH = 64
        EDGE_CH = 32
        key = jax.random.key(seed)
        ks = jax.random.split(key, 9)
        s = lambda d: 1.0 / np.sqrt(d)
        return {'x': jax.random.normal(ks[0], (N_NODES, IN_CH), dtype=jnp.float32), 'edge_index': jax.random.randint(ks[1], (2, N_EDGES), 0, N_NODES, dtype=jnp.int64 if jax.config.jax_enable_x64 else jnp.int32), 'edge_attr': jax.random.normal(ks[2], (N_EDGES, EDGE_CH), dtype=jnp.float32), 'We': jax.random.normal(ks[3], (IN_CH, EDGE_CH), dtype=jnp.float32) * s(EDGE_CH), 'be': jax.random.normal(ks[4], (IN_CH,), dtype=jnp.float32) * s(EDGE_CH), 'W1': jax.random.normal(ks[5], (OUT_CH, IN_CH), dtype=jnp.float32) * s(IN_CH), 'b1': jax.random.normal(ks[6], (OUT_CH,), dtype=jnp.float32) * s(IN_CH), 'W2': jax.random.normal(ks[7], (OUT_CH, OUT_CH), dtype=jnp.float32) * s(OUT_CH), 'b2': jax.random.normal(ks[8], (OUT_CH,), dtype=jnp.float32) * s(OUT_CH)}
    _L1_gnn_all = _L1_gnn_setup()
    _L1_gnn_in = {k: v for k, v in _L1_gnn_all.items() if k in ('We', 'be', 'W1', 'b1', 'W2', 'b2')}
    del _L1_gnn_all
    return {'x': x, 'src': src, 'dst': dst, 'edge_attr_32': edge_attr_32, 'L0_gnn_w_q': _L0_gnn_in['w_q'], 'L0_gnn_w_k': _L0_gnn_in['w_k'], 'L0_gnn_w_v': _L0_gnn_in['w_v'], 'L0_gnn_w_o': _L0_gnn_in['w_o'], 'L0_gnn_ln1_g': _L0_gnn_in['ln1_g'], 'L0_gnn_ln1_b': _L0_gnn_in['ln1_b'], 'L0_gnn_ln2_g': _L0_gnn_in['ln2_g'], 'L0_gnn_ln2_b': _L0_gnn_in['ln2_b'], 'L0_gnn_ff1_w': _L0_gnn_in['ff1_w'], 'L0_gnn_ff1_b': _L0_gnn_in['ff1_b'], 'L0_gnn_ff2_w': _L0_gnn_in['ff2_w'], 'L0_gnn_ff2_b': _L0_gnn_in['ff2_b'], 'L1_gnn_We': _L1_gnn_in['We'], 'L1_gnn_be': _L1_gnn_in['be'], 'L1_gnn_W1': _L1_gnn_in['W1'], 'L1_gnn_b1': _L1_gnn_in['b1'], 'L1_gnn_W2': _L1_gnn_in['W2'], 'L1_gnn_b2': _L1_gnn_in['b2']}

def reference(x, src, dst, edge_attr_32, L0_gnn_w_q, L0_gnn_w_k, L0_gnn_w_v, L0_gnn_w_o, L0_gnn_ln1_g, L0_gnn_ln1_b, L0_gnn_ln2_g, L0_gnn_ln2_b, L0_gnn_ff1_w, L0_gnn_ff1_b, L0_gnn_ff2_w, L0_gnn_ff2_b, L1_gnn_We, L1_gnn_be, L1_gnn_W1, L1_gnn_b1, L1_gnn_W2, L1_gnn_b2):
    import jax
    import jax.numpy as jnp

    def _L0_gnn_ref(x, edge_index, w_q, w_k, w_v, w_o, ln1_g, ln1_b, ln2_g, ln2_b, ff1_w, ff1_b, ff2_w, ff2_b):
        import jax, jax.numpy as jnp
        import numpy as np
        N = 3125
        E = 50000
        DIM = 64
        H = 4
        HD = DIM // H
        FF = 4 * DIM

        def _layernorm(x, g, b, eps=1e-05):
            m = x.mean(-1, keepdims=True)
            v = ((x - m) ** 2).mean(-1, keepdims=True)
            return (x - m) / jnp.sqrt(v + eps) * g + b
        row, col = (edge_index[0], edge_index[1])
        xn = _layernorm(x, ln1_g, ln1_b)
        Q = (xn @ w_q).reshape(N, H, HD)
        K = (xn @ w_k).reshape(N, H, HD)
        V = (xn @ w_v).reshape(N, H, HD)
        alpha = (Q[row] * K[col]).sum(-1) / np.sqrt(HD)
        a_exp = jnp.exp(alpha)
        denom = jax.ops.segment_sum(a_exp, row, num_segments=N)
        a = a_exp / (denom[row] + 1e-16)
        m = V[col] * a[:, :, None]
        out = jax.ops.segment_sum(m, row, num_segments=N).reshape(N, DIM)
        x = x + out @ w_o
        xn2 = _layernorm(x, ln2_g, ln2_b)
        ff = jax.nn.relu(xn2 @ ff1_w + ff1_b) @ ff2_w + ff2_b
        return x + ff

    def _L1_gnn_ref(x, edge_index, edge_attr, We, be, W1, b1, W2, b2):
        import jax, jax.numpy as jnp
        import numpy as np
        N_NODES = 50000
        N_EDGES = 25000
        IN_CH = 64
        OUT_CH = 64
        EDGE_CH = 32
        eps = jnp.float32(0.0)
        row, col = (edge_index[0], edge_index[1])
        edge_embedding = edge_attr @ We.T + be
        messages = jax.nn.relu(x[row] + edge_embedding)
        aggregated = jax.ops.segment_sum(messages, col, num_segments=x.shape[0])
        h = (1.0 + eps) * x + aggregated
        h = jax.nn.relu(h @ W1.T + b1)
        return h @ W2.T + b2
    edge_index = jnp.stack([src, dst])
    h = jnp.maximum(_layernorm(x, axis=-1), 0.0)
    x = x + _L0_gnn_ref(h, edge_index, L0_gnn_w_q, L0_gnn_w_k, L0_gnn_w_v, L0_gnn_w_o, L0_gnn_ln1_g, L0_gnn_ln1_b, L0_gnn_ln2_g, L0_gnn_ln2_b, L0_gnn_ff1_w, L0_gnn_ff1_b, L0_gnn_ff2_w, L0_gnn_ff2_b)
    h = jnp.maximum(_layernorm(x, axis=-1), 0.0)
    x = x + _L1_gnn_ref(h, edge_index, edge_attr_32, L1_gnn_We, L1_gnn_be, L1_gnn_W1, L1_gnn_b1, L1_gnn_W2, L1_gnn_b2)
    return x

_drawn_inputs = setup_inputs


def setup_inputs(seed=0):
    import zlib

    import numpy as np

    out = dict(_drawn_inputs(seed))
    spreads = {'L0_gnn_ln1_g': (1.0, 0.2),
     'L0_gnn_ln1_b': (0.0, 0.1),
     'L0_gnn_ln2_g': (1.0, 0.6),
     'L0_gnn_ln2_b': (0.0, 0.477),
     'L0_gnn_ff1_b': (0.0, 0.409),
     'L0_gnn_ff2_b': (0.0, 0.1)}
    factors = {'L1_gnn_b1': 4.455, 'L1_gnn_b2': 4.286}
    for name, (base, spread) in spreads.items():
        noise = np.random.default_rng([zlib.crc32(name.encode()), seed]).standard_normal(out[name].shape)
        drawn = base * np.exp(spread * noise) if base else spread * noise
        out[name] = jnp.asarray(drawn.astype(out[name].dtype))
    for name, factor in factors.items():
        out[name] = (out[name] * factor).astype(out[name].dtype)
    return out
```

```python
from contextlib import ExitStack

import concourse.bass as bass
from concourse import mybir

F32 = mybir.dt.float32
I32 = mybir.dt.int32
ALU = mybir.AluOpType
ACT = mybir.ActivationFunctionType
AX = mybir.AxisListType
ET = mybir.EngineType

N, D, H, FF, EC = 3125, 64, 4, 256, 32
E = 53125
HD = D // H
P = 128
NP, NT = 125, 25
TILES = -(-E // P)
G = 8
GROUPS = TILES // G
RING = 4
ROUNDS = GROUPS // RING
ACC_COLS = N + P
VD = D + H
EPS = 1e-5
DEN_EPS = 1e-16
assert TILES % G == 0 and GROUPS % RING == 0 and NP * NT == N

TB = 4
TBLOCKS = [range(a, min(a + TB, NT)) for a in range(0, NT, TB)]
QBLOCKS = [range(a, min(a + 2, NT)) for a in range(0, NT, 2)]
OBLOCKS = [range(a, min(a + 8, NT)) for a in range(0, NT, 8)]
CHUNKS = [(a, min(512, N - a)) for a in range(0, N, 512)]
NODE_JOBS = [("xnT", len(TBLOCKS), "A"), ("qkv", len(QBLOCKS), "AV"), ("den", len(CHUNKS), "V"),
             ("attn", len(OBLOCKS), "V"), ("xn2T", len(TBLOCKS), "A"), ("ff1", 2 * len(TBLOCKS), "A"),
             ("ff2", len(OBLOCKS), "V"), ("h1T", len(TBLOCKS), "A"), ("z1", len(CHUNKS), "A"),
             ("out", len(OBLOCKS), "V")]


def job_numbers():
    table, n, emptied = {}, 0, {"A": 0, "V": 0}
    for name, count, engines in NODE_JOBS:
        for k in range(count):
            emptied[engines[k % len(engines)]] += 1
            table[name, k] = (n, emptied["A"], emptied["V"])
            n += 1
    return table


def build(nc, x, srcg, dstT, dstrow, eaT, wqkv, wo, ff1w, ff1b, ff2w, weT, w1T, w2T, cols, rows,
          q_table, kv_table, h_table, out):
    jobs = job_numbers()
    by_number = {v[0]: v for v in jobs.values()}

    with ExitStack() as ctx:
        def sb(name, shape, dt=F32):
            return ctx.enter_context(nc.sbuf_tensor(name, shape, dt))

        def psum(name, shape):
            return ctx.enter_context(nc.psum_tensor(name, shape, F32))

        def sem(name):
            return ctx.enter_context(nc.semaphore(name))

        iota_w = sb("iota_w", [P, P])
        iota_p = sb("iota_p", [P, 1])
        ident = sb("ident", [P, P])
        ones_row = sb("ones_row", [1, P])
        head_rows = sb("head_rows", [P, D])
        eps_col = sb("eps_col", [P, 1])
        zeros = sb("zeros", [P, D])
        wqkv_sb = sb("wqkv_sb", [D, 3 * D])
        wo_sb = sb("wo_sb", [D, D])
        ff1w_sb = sb("ff1w_sb", [D, FF])
        ff2w_sb = sb("ff2w_sb", [P, 2, D])
        weT_sb = sb("weT_sb", [EC, D])
        w1T_sb = sb("w1T_sb", [D, D])
        w2T_sb = sb("w2T_sb", [D, D])
        cols_sb = sb("cols_sb", [D, 5])
        ff1b_sb = sb("ff1b_sb", [P, 2])
        rows_sb = sb("rows_sb", [1, 2, D])
        be_sb = sb("be_sb", [P, D])
        dstT_i = sb("dstT_i", [P, TILES], I32)
        base_i = sb("base_i", [P, TILES], I32)
        base_f = sb("base_f", [P, TILES])
        rel = sb("rel", [P, TILES])
        window_node = sb("window_node", [P, TILES])
        x_sb = sb("x_sb", [NP, NT, D])
        h_sb = sb("h_sb", [NP, NT, D])
        cen = sb("cen", [NP, NT, D])
        q_sb = sb("q_sb", [NP, NT, D])
        sq = q_sb
        kv_sb = sb("kv_sb", [NP, NT, 2 * D])
        x1_sb = sb("x1_sb", [NP, NT, D])
        stat = sb("stat", [NP, 5, NT])
        xnT = sb("xnT", [D, N])
        acc = sb("acc", [P, ACC_COLS])
        mT = sb("mT", [D, N])
        rec = xnT
        ffT = sb("ffT", [P, 2, N])
        idx = [sb(f"idx{b}", [P, G], I32) for b in range(RING)]
        kv = [sb(f"kv{b}", [P, G, 2 * D]) for b in range(RING)]
        qwin = [sb(f"qwin{b}", [P, G, D]) for b in range(RING)]
        drow = [sb(f"drow{b}", [P, G * P], I32) for b in range(RING)]
        ea = [sb(f"ea{b}", [EC, G, P]) for b in range(RING)]
        spread = [sb(f"spread{b}", [P, G, P]) for b in range(2)]
        collect = [sb(f"collect{b}", [P, G, P]) for b in range(2)]
        prod = [sb(f"prod{b}", [P, G, D]) for b in range(2)]
        alpha = [sb(f"alpha{b}", [P, G * H]) for b in range(2)]
        vals = [sb(f"vals{b}", [P, G, VD]) for b in range(2)]

        ps_edge = [psum(f"ps_edge{b}", [P, 512]) for b in range(2)]
        ps_sum = [psum(f"ps_sum{b}", [P, G * P]) for b in range(2)]
        ps_node = [psum(f"ps_node{b}", [P, 512]) for b in range(2)]
        banks = ps_node + ps_edge

        x_landed = sem("x_landed")
        weights_landed = sem("weights_landed")
        dst_landed = sem("dst_landed")
        tables_stored = sem("tables_stored")
        h_stored = sem("h_stored")
        out_stored = sem("out_stored")
        idx_landed = [sem(f"idx_landed{b}") for b in range(RING)]
        kv_landed = [sem(f"kv_landed{b}") for b in range(RING)]
        qwin_landed = [sem(f"qwin_landed{b}") for b in range(RING)]
        drow_landed = [sem(f"drow_landed{b}") for b in range(RING)]
        ea_landed = [sem(f"ea_landed{b}") for b in range(RING)]
        hg_landed = [sem(f"hg_landed{b}") for b in range(RING)]
        gathers_begun = sem("gathers_begun")
        iotas_made = sem("iotas_made")
        consts_made = sem("consts_made")
        windows_made = sem("windows_made")
        acc_cleared = sem("acc_cleared")
        dve_chain = sem("dve_chain")
        act_chain = sem("act_chain")
        variance_ready = sem("variance_ready")
        deviation_ready = sem("deviation_ready")
        normed = sem("normed")
        bank_filled = sem("bank_filled")
        emptied_act = sem("emptied_act")
        emptied_dve = sem("emptied_dve")
        attended = sem("attended")
        spread_made = sem("spread_made")
        spread_used = sem("spread_used")
        collect_made = sem("collect_made")
        prod_made = sem("prod_made")
        alpha_made = sem("alpha_made")
        exp_made = sem("exp_made")
        vals_made = sem("vals_made")
        summed = sem("summed")
        added = sem("added")
        emb_made = sem("emb_made")
        collect1_made = sem("collect1_made")
        message_made = sem("message_made")
        relu_made = sem("relu_made")
        summed1 = sem("summed1")
        added1 = sem("added1")

        def rounds(engine, body):
            body(0, True, False)
            with engine.Fori(1, ROUNDS - 1) as r:
                body(r, False, False)
            body(ROUNDS - 1, False, True)

        def by_nodes(engine, dst_rows, src_rows, signal, partitions=(0, 112, NP)):
            for a, b in zip(partitions, partitions[1:]):
                engine.dma_start(dst_rows[a:b], src_rows[a:b]).then_inc(signal, 16)

        def dram_nodes(table, width):
            return table[0:N, 0:width].rearrange("(p t) d -> p (t d)", t=NT)

        block = ctx.enter_context(nc.Block())

        @block.sync
        def _(sp):
            by_nodes(sp, x_sb[:, :, :].rearrange("p t d -> p (t d)"), dram_nodes(x, D), x_landed)
            sp.dma_start(dstT_i[:, :], dstT[:, :]).then_inc(dst_landed, 16)
            sp.dma_start(base_i[:, :], dstT[0:1, :].partition_broadcast(P)).then_inc(dst_landed, 16)
            for b in range(RING):
                sp.dma_start(idx[b][:, :], srcg[b]).then_inc(idx_landed[b], 16)
                sp.dma_start(drow[b][:, :], dstrow[b:b + 1, :].partition_broadcast(P)).then_inc(drow_landed[b], 16)
                sp.dma_start(ea[b][:, :, :], eaT[b]).then_inc(ea_landed[b], 16)

            _, n_act, n_dve = jobs["qkv", len(QBLOCKS) - 1]
            sp.wait_ge(consts_made, 1)
            sp.dma_start(q_table[N:N + P, :], zeros[:, :]).then_inc(tables_stored, 16)
            sp.wait_ge(emptied_act, n_act)
            sp.wait_ge(emptied_dve, n_dve)
            by_nodes(sp, dram_nodes(q_table, D), q_sb[:, :, :].rearrange("p t d -> p (t d)"), tables_stored)
            by_nodes(sp, dram_nodes(kv_table, 2 * D), kv_sb[:, :, :].rearrange("p t d -> p (t d)"), tables_stored)

            def load_windows(group, b):
                _, bases = nc.values_load_multi_w_load_instructions(
                    base_i[0:1, bass.ds(group * G, G)], engines=[ET.SP], min_val=0, max_val=N - 1,
                    skip_runtime_bounds_check_because="dst is a node's number, the first of a tile never padding")
                for j in range(G):
                    sp.dma_start(qwin[b][:, j, :], q_table[bass.ds(bases[j], P), :]).then_inc(qwin_landed[b], 16)

            sp.wait_ge(tables_stored, 16 * 5)
            sp.wait_ge(dst_landed, 32)
            for b in range(RING):
                load_windows(b, b)

            def next_inputs(r, first, last):
                if last:
                    return
                for b in range(RING):
                    group = r * RING + b
                    sp.wait_ge(kv_landed[b], 16 * G * (r + 1))
                    sp.dma_start(idx[b][:, :], srcg[bass.ds(group + RING, 1)].rearrange("a p j -> (a p) j")
                                 ).then_inc(idx_landed[b], 16)
                    sp.wait_ge(spread_made, group + 1)
                    sp.dma_start(drow[b][:, :], dstrow[bass.ds(group + RING, 1), :].partition_broadcast(P)
                                 ).then_inc(drow_landed[b], 16)
                    sp.wait_ge(spread_used, group + 1)
                    load_windows(group + RING, b)

            rounds(sp, next_inputs)

            for b in range(RING):
                sp.wait_ge(kv_landed[b], 16 * G * ROUNDS)
                sp.dma_start(idx[b][:, :], srcg[b]).then_inc(idx_landed[b], 16)

            sp.wait_ge(normed, 4)
            by_nodes(sp, dram_nodes(h_table, D), q_sb[:, :, :].rearrange("p t d -> p (t d)"), h_stored)

            def next_inputs1(r, first, last):
                if last:
                    return
                for b in range(RING):
                    group = r * RING + b
                    sp.wait_ge(hg_landed[b], 16 * G * (r + 1))
                    sp.dma_start(idx[b][:, :], srcg[bass.ds(group + RING, 1)].rearrange("a p j -> (a p) j")
                                 ).then_inc(idx_landed[b], 16)
                    sp.wait_ge(emb_made, group + 1)
                    sp.dma_start(ea[b][:, :, :], eaT[bass.ds(group + RING, 1)].rearrange("a c j e -> (a c) j e")
                                 ).then_inc(ea_landed[b], 16)

            rounds(sp, next_inputs1)

            out_rows = out[:, :].rearrange("(p t) d -> p t d", t=NT)
            for k, block_range in enumerate(OBLOCKS):
                a, b = block_range[0], block_range[-1] + 1
                sp.wait_ge(emptied_dve, jobs["out", k][2])
                by_nodes(sp, out_rows[:, a:b, :], h_sb[:, a:b, :], out_stored)
            sp.wait_ge(out_stored, 32 * len(OBLOCKS))

        @block.gpsimd
        def _(pool):
            nc.gpsimd.iota(iota_w[:, :], [[1, P]], base=0, channel_multiplier=0,
                           allow_small_or_imprecise_dtypes=True).then_inc(iotas_made, 1)
            nc.gpsimd.iota(iota_p[:, :], [[0, 1]], base=0, channel_multiplier=1,
                           allow_small_or_imprecise_dtypes=True).then_inc(iotas_made, 1)

            def gather(r, b, table, width, landed):
                for j in range(G):
                    pool.indirect_dma_start(
                        out=kv[b][:, j, 0:width], out_offset=None, in_=table,
                        in_offset=bass.IndirectOffsetOnAxis(ap=idx[b][:, j:j + 1], axis=0)).then_inc(landed[b], 16)

            def gather_kv(r, first, last):
                for b in range(RING):
                    pool.wait_ge(idx_landed[b], 16 * (r + 1))
                    if not first:
                        pool.wait_ge(vals_made, (r - 1) * RING + b + 1)
                    pool.sem_inc(gathers_begun, 1)
                    gather(r, b, kv_table[:, :], 2 * D, kv_landed)

            pool.wait_ge(tables_stored, 16 * 5)
            rounds(pool, gather_kv)

            def gather_h(r, first, last):
                for b in range(RING):
                    pool.wait_ge(idx_landed[b], 16 * (ROUNDS + r + 1))
                    if not first:
                        pool.wait_ge(message_made, (r - 1) * RING + b + 1)
                    pool.sem_inc(gathers_begun, 1)
                    gather(r, b, h_table[:, :], D, hg_landed)

            pool.wait_ge(h_stored, 32)
            rounds(pool, gather_h)

        @block.tensor
        def _(pe):
            def bank_of(name, k):
                n = jobs[name, k][0]
                if n >= len(banks):
                    _, n_act, n_dve = by_number[n - len(banks)]
                    if n_act:
                        pe.wait_ge(emptied_act, n_act)
                    if n_dve:
                        pe.wait_ge(emptied_dve, n_dve)
                return banks[n % len(banks)]

            def transposes(name, source):
                for k, ts in enumerate(TBLOCKS):
                    bank = bank_of(name, k)
                    for i, t in enumerate(ts):
                        last = nc.tensor.transpose(bank[0:D, i * NP:(i + 1) * NP], source[:, t, :],
                                                   ident[0:NP, 0:NP])
                    last.then_inc(bank_filled, 1)

            pe.wait_ge(consts_made, 1)
            pe.wait_ge(weights_landed, 16 * WEIGHT_DMAS)
            pe.wait_ge(normed, 1)
            transposes("xnT", cen)

            for k, ts in enumerate(QBLOCKS):
                bank = bank_of("qkv", k)
                pe.wait_ge(emptied_act, jobs["xnT", ts[-1] // TB][1])
                for i, t in enumerate(ts):
                    last = nc.tensor.matmul(bank[0:NP, i * 3 * D:(i + 1) * 3 * D], xnT[:, t * NP:(t + 1) * NP],
                                            wqkv_sb[:, :], start=True, stop=True)
                last.then_inc(bank_filled, 1)

            def expand(r, b, first):
                group = r * RING + b
                pe.wait_ge(spread_made, group + 1)
                pe.wait_ge(qwin_landed[b], 16 * G * (r + 1))
                if not (first and b < 2):
                    pe.wait_ge(prod_made, group - 1)
                for j in range(G):
                    last = nc.tensor.matmul(ps_edge[b % 2][:, j * D:(j + 1) * D], spread[b % 2][:, j, :],
                                            qwin[b][:, j, :], start=True, stop=True)
                last.then_inc(spread_used, 1)

            def edges0(r, first, last_round):
                if first:
                    expand(0, 0, True)
                for b in range(RING):
                    group = r * RING + b
                    if b + 1 < RING:
                        expand(r, b + 1, first)
                    elif not last_round:
                        expand(r + 1, 0, False)
                    pe.wait_ge(vals_made, group + 1)
                    pe.wait_ge(collect_made, group + 1)
                    if not (first and b < 2):
                        pe.wait_ge(added, G * (group - 1))
                    for j in range(G):
                        last = nc.tensor.matmul(ps_sum[b % 2][0:VD, j * P:(j + 1) * P], vals[b % 2][:, j, :],
                                                collect[b % 2][:, j, :], start=True, stop=True)
                    last.then_inc(summed, 1)

            pe.wait_ge(emptied_act, jobs["qkv", len(QBLOCKS) - 1][1])
            pe.wait_ge(emptied_dve, jobs["qkv", len(QBLOCKS) - 1][2])
            rounds(pe, edges0)

            pe.wait_ge(added, G * GROUPS)
            for k, (a, w) in enumerate(CHUNKS):
                bank = bank_of("den", k)
                nc.tensor.matmul(bank[0:D, 0:w], head_rows[D:VD, :], acc[D:VD, a:a + w],
                                 start=True, stop=True).then_inc(bank_filled, 1)
            pe.wait_ge(attended, len(CHUNKS))
            for k, ts in enumerate(OBLOCKS):
                bank = bank_of("attn", k)
                for i, t in enumerate(ts):
                    last = nc.tensor.matmul(bank[0:NP, i * D:(i + 1) * D], mT[:, t:N:NT], wo_sb[:, :],
                                            start=True, stop=True)
                last.then_inc(bank_filled, 1)
            pe.wait_ge(normed, 2)
            transposes("xn2T", cen)
            for k in range(2 * len(TBLOCKS)):
                ts, half = TBLOCKS[k // 2], k % 2
                bank = bank_of("ff1", k)
                pe.wait_ge(emptied_act, jobs["xn2T", k // 2][1])
                cols = slice(ts[0] * NP, (ts[-1] + 1) * NP)
                nc.tensor.matmul(bank[:, 0:len(ts) * NP], ff1w_sb[:, half * P:(half + 1) * P], xnT[:, cols],
                                 start=True, stop=True).then_inc(bank_filled, 1)
            for k, ts in enumerate(OBLOCKS):
                bank = bank_of("ff2", k)
                pe.wait_ge(emptied_act, jobs["ff1", 2 * (ts[-1] // TB) + 1][1])
                for i, t in enumerate(ts):
                    for half in range(2):
                        nc.tensor.matmul(bank[0:NP, i * D:(i + 1) * D], ffT[:, half, t * NP:(t + 1) * NP],
                                         ff2w_sb[:, half, :], start=(half == 0), stop=False)
                    last = nc.tensor.matmul(bank[0:NP, i * D:(i + 1) * D], ones_row[:, 0:NP], rows_sb[:, 0, :],
                                            start=False, stop=True)
                last.then_inc(bank_filled, 1)
            pe.wait_ge(normed, 3)
            transposes("h1T", h_sb)

            def embed(r, b, first):
                group = r * RING + b
                pe.wait_ge(ea_landed[b], 16 * (r + 1))
                if not (first and b < 2):
                    pe.wait_ge(message_made, group - 1)
                for j in range(G):
                    last = nc.tensor.matmul(ps_edge[b % 2][:, j * D:(j + 1) * D], ea[b][:, j, :],
                                            weT_sb[:, :], start=True, stop=True)
                last.then_inc(emb_made, 1)

            def edges1(r, first, last_round):
                if first:
                    embed(0, 0, True)
                for b in range(RING):
                    group = r * RING + b
                    if b + 1 < RING:
                        embed(r, b + 1, first)
                    elif not last_round:
                        embed(r + 1, 0, False)
                    pe.wait_ge(relu_made, group + 1)
                    pe.wait_ge(collect1_made, group + 1)
                    if not (first and b < 2):
                        pe.wait_ge(added1, G * (group - 1))
                    for j in range(G):
                        last = nc.tensor.matmul(ps_sum[b % 2][0:D, j * P:(j + 1) * P], vals[b % 2][:, j, 0:D],
                                                collect[b % 2][:, j, :], start=True, stop=True)
                    last.then_inc(summed1, 1)

            pe.wait_ge(emptied_act, jobs["h1T", len(TBLOCKS) - 1][1])
            rounds(pe, edges1)

            pe.wait_ge(added1, G * GROUPS)
            for k, (a, w) in enumerate(CHUNKS):
                bank = bank_of("z1", k)
                nc.tensor.matmul(bank[0:D, 0:w], w1T_sb[:, :], acc[0:D, a:a + w],
                                 start=True, stop=True).then_inc(bank_filled, 1)
            pe.wait_ge(emptied_act, jobs["z1", len(CHUNKS) - 1][1])
            for k, ts in enumerate(OBLOCKS):
                bank = bank_of("out", k)
                for i, t in enumerate(ts):
                    nc.tensor.matmul(bank[0:NP, i * D:(i + 1) * D], mT[:, t:N:NT], w2T_sb[:, :],
                                     start=True, stop=False)
                    last = nc.tensor.matmul(bank[0:NP, i * D:(i + 1) * D], ones_row[:, 0:NP], rows_sb[:, 1, :],
                                            start=False, stop=True)
                last.then_inc(bank_filled, 1)

        @block.scalar
        def _(act):
            def load(dst, src):
                act.dma_start(dst, src).then_inc(weights_landed, 16)

            load(wqkv_sb[:, :], wqkv[:, :])
            load(wo_sb[:, :], wo[:, :])
            load(ff1w_sb[:, :], ff1w[:, :])
            load(ff2w_sb[:, :, :], ff2w[:, :].rearrange("(c p) n -> p c n", p=P))
            load(weT_sb[:, :], weT[:, :])
            load(w1T_sb[:, :], w1T[:, :])
            load(w2T_sb[:, :], w2T[:, :])
            load(cols_sb[:, :], cols[:, :])
            load(ff1b_sb[:, :], ff1b[:, :])
            load(rows_sb[:, :, :], rows[0:1, 0:2])
            load(be_sb[:, :], rows[0, 2:3].partition_broadcast(P))

            def deviation(n):
                act.wait_ge(variance_ready, n + 1)
                if n == 0:
                    act.wait_ge(consts_made, 1)
                nc.scalar.activation(stat[:, 3, :], stat[:, 2, :], ACT.Sqrt, bias=eps_col[0:NP, :],
                                     scale=1.0 / D).then_inc(deviation_ready, 1)

            def filled(name, k):
                n = jobs[name, k][0]
                act.wait_ge(bank_filled, n + 1)
                return banks[n % len(banks)]

            def scaled_transposes(name, g, b):
                for k, ts in enumerate(TBLOCKS):
                    bank = filled(name, k)
                    nc.scalar.activation(xnT[:, ts[0] * NP:(ts[-1] + 1) * NP], bank[0:D, 0:len(ts) * NP],
                                         ACT.Identity, bias=cols_sb[:, b:b + 1], scale=cols_sb[:, g:g + 1]
                                         ).then_inc(emptied_act, 1)

            deviation(0)
            deviation(1)
            act.wait_ge(weights_landed, 16 * WEIGHT_DMAS)
            scaled_transposes("xnT", 0, 1)
            for k, ts in list(enumerate(QBLOCKS))[0::2]:
                bank = filled("qkv", k)
                view = bank[0:NP, 0:len(ts) * 3 * D].rearrange("p (t c) -> p t c", c=3 * D)
                nc.scalar.activation(q_sb[:, ts[0]:ts[-1] + 1, :], view[:, :, 0:D], ACT.Copy, scale=HD ** -0.5)
                nc.scalar.activation(kv_sb[:, ts[0]:ts[-1] + 1, :], view[:, :, D:3 * D],
                                     ACT.Copy).then_inc(emptied_act, 1)

            def exps(r, first, last):
                for b in range(RING):
                    group = r * RING + b
                    act.wait_ge(alpha_made, group + 1)
                    if not (first and b < 2):
                        act.wait_ge(summed, group - 1)
                    nc.scalar.activation(vals[b % 2][:, :, D:VD],
                                         alpha[b % 2][:, :].rearrange("p (j h) -> p j h", h=H),
                                         ACT.Exp).then_inc(exp_made, 1)

            rounds(act, exps)

            deviation(2)
            scaled_transposes("xn2T", 2, 3)
            for k in range(2 * len(TBLOCKS)):
                ts, half = TBLOCKS[k // 2], k % 2
                bank = filled("ff1", k)
                nc.scalar.activation(ffT[:, half, ts[0] * NP:(ts[-1] + 1) * NP], bank[:, 0:len(ts) * NP], ACT.Relu,
                                     bias=ff1b_sb[:, half:half + 1]).then_inc(emptied_act, 1)
            deviation(3)
            for k, ts in enumerate(TBLOCKS):
                bank = filled("h1T", k)
                nc.scalar.activation(acc[0:D, 0:N].rearrange("d (p t) -> d t p", t=NT)[:, ts[0]:ts[-1] + 1, :],
                                     bank[0:D, 0:len(ts) * NP].rearrange("d (t p) -> d t p", p=NP),
                                     ACT.Copy).then_inc(emptied_act, 1)

            def relus(r, first, last):
                for b in range(RING):
                    group = r * RING + b
                    act.wait_ge(message_made, group + 1)
                    if not (first and b < 2):
                        act.wait_ge(summed1, group - 1)
                    nc.scalar.activation(vals[b % 2][:, :, 0:D], prod[b % 2][:, :, :],
                                         ACT.Relu).then_inc(relu_made, 1)

            rounds(act, relus)

            for k, (a, w) in enumerate(CHUNKS):
                bank = filled("z1", k)
                nc.scalar.activation(mT[:, a:a + w], bank[0:D, 0:w], ACT.Relu,
                                     bias=cols_sb[:, 4:5]).then_inc(emptied_act, 1)

        @block.vector
        def _(dve):
            done = [0]

            def link(ins):
                done[0] += 1
                ins.then_inc(dve_chain, 1)
                dve.wait_ge(dve_chain, done[0])

            dve.wait_ge(iotas_made, 2)
            nc.vector.memset(acc[:, :], 0.0).then_inc(acc_cleared, 1)
            nc.vector.memset(eps_col[:, :], EPS)
            nc.vector.memset(zeros[:, :], 0.0)
            nc.vector.memset(ones_row[:, :], 1.0)
            link(nc.vector.tensor_tensor(ident[:, :], iota_w[:, :], iota_p[:, 0:1].to_broadcast([P, P]),
                                         ALU.is_equal))
            nc.vector.tensor_copy(head_rows[:, :].rearrange("p (h c) -> p h c", c=HD),
                                  ident[:, D:VD].unsqueeze(2).to_broadcast([P, H, HD])).then_inc(consts_made, 1)
            dve.wait_ge(acc_cleared, 1)
            link(nc.vector.memset(acc[D:VD, :], DEN_EPS))

            def normalise(n, source, result, op0, scalar):
                link(nc.vector.tensor_reduce(stat[:, 0, :], source[:, :, :], AX.X, ALU.add))
                link(nc.vector.tensor_scalar(stat[:, 1, :], stat[:, 0, :], 1.0 / D, None, ALU.mult))
                link(nc.vector.tensor_tensor(cen[:, :, :], source[:, :, :],
                                             stat[:, 1, :].unsqueeze(2).to_broadcast([NP, NT, D]), ALU.subtract))
                link(nc.vector.tensor_tensor(sq[:, :, :], cen[:, :, :], cen[:, :, :], ALU.mult))
                nc.vector.tensor_reduce(stat[:, 2, :], sq[:, :, :], AX.X, ALU.add).then_inc(variance_ready, 1)
                dve.wait_ge(deviation_ready, n + 1)
                link(nc.vector.reciprocal(stat[:, 4, :], stat[:, 3, :]))
                return nc.vector.scalar_tensor_tensor(result[:, :, :], cen[:, :, :], scalar,
                                                      stat[:, 4, :].unsqueeze(2).to_broadcast([NP, NT, D]),
                                                      op0, ALU.mult)

            def filled(name, k):
                n = jobs[name, k][0]
                dve.wait_ge(bank_filled, n + 1)
                return banks[n % len(banks)]

            dve.wait_ge(x_landed, 32)
            link(normalise(0, x_sb, h_sb, ALU.max, 0.0))
            normalise(1, h_sb, cen, ALU.mult, 1.0).then_inc(normed, 1)

            dve.wait_ge(dst_landed, 32)
            link(nc.vector.tensor_copy(base_f[:, :], base_i[:, :]))
            nc.vector.tensor_tensor(rel[:, :], dstT_i[:, :], base_f[:, :], ALU.subtract)
            link(nc.vector.tensor_scalar(window_node[:, :], base_f[:, :], iota_p[:, 0:1], None, ALU.add))

            for k, ts in list(enumerate(QBLOCKS))[1::2]:
                bank = filled("qkv", k)
                view = bank[0:NP, 0:len(ts) * 3 * D].rearrange("p (t c) -> p t c", c=3 * D)
                nc.vector.tensor_scalar(q_sb[:, ts[0]:ts[-1] + 1, :], view[:, :, 0:D], HD ** -0.5, None, ALU.mult)
                nc.vector.tensor_copy(kv_sb[:, ts[0]:ts[-1] + 1, :], view[:, :, D:3 * D]).then_inc(emptied_dve, 1)

            def make_spread(r, b, first):
                group = r * RING + b
                dve.wait_ge(drow_landed[b], 16 * (r + 1))
                if not (first and b < 2):
                    dve.wait_ge(spread_used, group - 1)
                nc.vector.tensor_tensor(spread[b % 2][:, :, :], drow[b][:, :].rearrange("p (j e) -> p j e", e=P),
                                        window_node[:, bass.ds(group * G, G)].unsqueeze(2).to_broadcast([P, G, P]),
                                        ALU.is_equal).then_inc(spread_made, 1)

            def make_collect(r, b, first, used, made):
                group = r * RING + b
                if not (first and b < 2):
                    dve.wait_ge(used, group - 1)
                nc.vector.tensor_tensor(collect[b % 2][:, :, :],
                                        iota_w[:, :].unsqueeze(1).to_broadcast([P, G, P]),
                                        rel[:, bass.ds(group * G, G)].unsqueeze(2).to_broadcast([P, G, P]),
                                        ALU.is_equal).then_inc(made, 1)

            def add_windows(group, b, rows, was_summed, was_added, none_before):
                _, bases = nc.values_load_multi_w_load_instructions(
                    base_i[0:1, bass.ds(group * G, G)], engines=[ET.DVE], min_val=0, max_val=N - 1,
                    skip_runtime_bounds_check_because="dst is a node's number, the first of a tile never padding")
                dve.wait_ge(was_summed, group + 1)
                for j in range(G):
                    if not (none_before and j == 0):
                        dve.wait_ge(was_added, group * G + j)
                    window = acc[0:rows, bass.ds(bases[j], P)]
                    nc.vector.tensor_tensor(window, window, ps_sum[b % 2][0:rows, j * P:(j + 1) * P],
                                            ALU.add).then_inc(was_added, 1)

            def edges0(r, first, last_round):
                if first:
                    make_spread(0, 0, True)
                for b in range(RING):
                    group = r * RING + b
                    if b + 1 < RING:
                        make_spread(r, b + 1, first)
                    elif not last_round:
                        make_spread(r + 1, 0, False)
                    make_collect(r, b, first, summed, collect_made)
                    dve.wait_ge(kv_landed[b], 16 * G * (r + 1))
                    dve.wait_ge(spread_used, group + 1)
                    nc.vector.tensor_tensor(prod[b % 2][:, :, :],
                                            ps_edge[b % 2][:, :].rearrange("p (j c) -> p j c", c=D),
                                            kv[b][:, :, 0:D], ALU.mult).then_inc(prod_made, 1)
                    dve.wait_ge(prod_made, group + 1)
                    if not (first and b < 2):
                        dve.wait_ge(exp_made, group - 1)
                    nc.vector.tensor_reduce(alpha[b % 2][:, :],
                                            prod[b % 2][:, :, :].rearrange("p j (h c) -> p (j h) c", c=HD),
                                            AX.X, ALU.add).then_inc(alpha_made, 1)
                    if not (first and b == 0):
                        add_windows(group - 1, (b - 1) % 2, VD, summed, added, first and b == 1)
                    dve.wait_ge(exp_made, group + 1)
                    nc.vector.tensor_tensor(vals[b % 2][:, :, 0:D].rearrange("p j (h c) -> p j h c", c=HD),
                                            kv[b][:, :, D:2 * D].rearrange("p j (h c) -> p j h c", c=HD),
                                            vals[b % 2][:, :, D:VD].unsqueeze(3).to_broadcast([P, G, H, HD]),
                                            ALU.mult).then_inc(vals_made, 1)

            rounds(dve, edges0)
            add_windows(GROUPS - 1, (RING - 1) % 2, VD, summed, added, False)

            dve.wait_ge(added, G * GROUPS)
            for k, (a, w) in enumerate(CHUNKS):
                bank = filled("den", k)
                nc.vector.reciprocal(rec[:, a:a + w], bank[0:D, 0:w]).then_inc(emptied_dve, 1)
                dve.wait_ge(emptied_dve, jobs["den", k][2])
                nc.vector.tensor_tensor(mT[:, a:a + w], acc[0:D, a:a + w], rec[:, a:a + w],
                                        ALU.mult).then_inc(attended, 1)
            for k, ts in enumerate(OBLOCKS):
                bank = filled("attn", k)
                nc.vector.tensor_tensor(x1_sb[:, ts[0]:ts[-1] + 1, :],
                                        bank[0:NP, 0:len(ts) * D].rearrange("p (t d) -> p t d", d=D),
                                        h_sb[:, ts[0]:ts[-1] + 1, :], ALU.add).then_inc(emptied_dve, 1)
            dve.wait_ge(emptied_dve, jobs["attn", len(OBLOCKS) - 1][2])
            normalise(2, x1_sb, cen, ALU.mult, 1.0).then_inc(normed, 1)
            link(nc.vector.tensor_tensor(x1_sb[:, :, :], x1_sb[:, :, :], x_sb[:, :, :], ALU.add))
            for k, ts in enumerate(OBLOCKS):
                bank = filled("ff2", k)
                nc.vector.tensor_tensor(x_sb[:, ts[0]:ts[-1] + 1, :],
                                        bank[0:NP, 0:len(ts) * D].rearrange("p (t d) -> p t d", d=D),
                                        x1_sb[:, ts[0]:ts[-1] + 1, :], ALU.add).then_inc(emptied_dve, 1)
            dve.wait_ge(emptied_dve, jobs["ff2", len(OBLOCKS) - 1][2])
            normalise(3, x_sb, h_sb, ALU.max, 0.0).then_inc(normed, 1)
            dve.wait_ge(normed, 3)
            nc.vector.tensor_tensor(q_sb[:, :, :], h_sb[:, :, :],
                                    be_sb[0:NP, :].unsqueeze(1).to_broadcast([NP, NT, D]),
                                    ALU.add).then_inc(normed, 1)

            dve.wait_ge(emptied_act, jobs["h1T", len(TBLOCKS) - 1][1])

            def edges1(r, first, last_round):
                for b in range(RING):
                    group = r * RING + b
                    make_collect(r, b, first, summed1, collect1_made)
                    dve.wait_ge(hg_landed[b], 16 * G * (r + 1))
                    dve.wait_ge(emb_made, group + 1)
                    if not (first and b < 2):
                        dve.wait_ge(relu_made, group - 1)
                    nc.vector.tensor_tensor(prod[b % 2][:, :, :],
                                            ps_edge[b % 2][:, :].rearrange("p (j c) -> p j c", c=D),
                                            kv[b][:, :, 0:D], ALU.add).then_inc(message_made, 1)
                    if not (first and b == 0):
                        add_windows(group - 1, (b - 1) % 2, D, summed1, added1, first and b == 1)

            rounds(dve, edges1)
            add_windows(GROUPS - 1, (RING - 1) % 2, D, summed1, added1, False)

            for k, ts in enumerate(OBLOCKS):
                bank = filled("out", k)
                nc.vector.tensor_tensor(h_sb[:, ts[0]:ts[-1] + 1, :],
                                        bank[0:NP, 0:len(ts) * D].rearrange("p (t d) -> p t d", d=D),
                                        x_sb[:, ts[0]:ts[-1] + 1, :], ALU.add).then_inc(emptied_dve, 1)


WEIGHT_DMAS = 11


def kernel(**inputs):
    import numpy as _np
    import concourse.bacc as _bacc
    from concourse import mybir as _mybir
    from concourse.bass_utils import run_bass_kernel_spmd as _run

    a = {k: _np.asarray(v) for k, v in inputs.items()}
    edges = TILES * P

    def padded(v, fill):
        return _np.concatenate([v, _np.full((edges - E,) + v.shape[1:], fill, v.dtype)])

    src, dst = padded(a["src"], 0), padded(a["dst"], -1)
    edge_attr = padded(a["edge_attr_32"], 0)
    wqkv = _np.concatenate([a["L0_gnn_w_q"], a["L0_gnn_w_k"], a["L0_gnn_w_v"]], axis=1)
    laid = {
        "x": a["x"],
        "srcg": src.reshape(GROUPS, G, P).transpose(0, 2, 1),
        "dstT": dst.reshape(TILES, P).T,
        "dstrow": dst.reshape(GROUPS, G * P),
        "eaT": edge_attr.reshape(GROUPS, G, P, EC).transpose(0, 3, 1, 2),
        "wqkv": wqkv,
        "wo": a["L0_gnn_w_o"],
        "ff1w": a["L0_gnn_ff1_w"], "ff1b": a["L0_gnn_ff1_b"].reshape(2, P).T, "ff2w": a["L0_gnn_ff2_w"],
        "weT": a["L1_gnn_We"].T,
        "w1T": a["L1_gnn_W1"].T, "w2T": a["L1_gnn_W2"].T,
        "cols": _np.stack([a["L0_gnn_ln1_g"], a["L0_gnn_ln1_b"], a["L0_gnn_ln2_g"], a["L0_gnn_ln2_b"],
                           a["L1_gnn_b1"]], axis=1),
        "rows": _np.stack([a["L0_gnn_ff2_b"], a["L1_gnn_b2"], a["L1_gnn_be"]])[None],
    }
    nc = _bacc.Bacc("TRN2", target_bir_lowering=False, num_devices=1)
    arrays, args = {}, []
    for name, v in laid.items():
        v = _np.ascontiguousarray(v)
        arrays[f"in_{name}"] = v
        args.append(nc.dram_tensor(f"in_{name}", v.shape, _mybir.dt.from_np(v.dtype), kind="ExternalInput").ap())
    f32 = _mybir.dt.float32
    tables = [nc.dram_tensor("q_table", (ACC_COLS, D), f32, kind="Internal").ap(),
              nc.dram_tensor("kv_table", (N, 2 * D), f32, kind="Internal").ap(),
              nc.dram_tensor("h_table", (N, D), f32, kind="Internal").ap()]
    out = nc.dram_tensor("out_0", (N, D), f32, kind="ExternalOutput").ap()
    build(nc, *args, *tables, out)
    r = _run(nc, [arrays], core_ids=[0])
    return r.results[0]["out_0"]
```

```python
from contextlib import ExitStack

import concourse.bass as bass
from concourse import mybir

F32 = mybir.dt.float32
BF16 = mybir.dt.bfloat16
I32 = mybir.dt.int32
ALU = mybir.AluOpType
ACT = mybir.ActivationFunctionType
AX = mybir.AxisListType
ET = mybir.EngineType

N, D, H, FF, EC = 3125, 64, 4, 256, 32
E = 53125
HD = D // H
P = 128
NP, NT = 125, 25
TILES = -(-E // P)
G = 8
GROUPS = TILES // G
RING = 4
ROUNDS = GROUPS // RING
ACC_COLS = N + P
VD = D + H
EPS = 1e-5
DEN_EPS = 1e-16
assert TILES % G == 0 and GROUPS % RING == 0 and NP * NT == N

HALVES = [range(0, 13), range(13, NT)]


def blocks_of(size):
    return [(half, range(a, min(a + size, ts.stop))) for half, ts in enumerate(HALVES)
            for a in range(ts.start, ts.stop, size)]


TBLOCKS = blocks_of(4)
QBLOCKS = blocks_of(2)
OBLOCKS = blocks_of(8)
JOBS = {"xnT": TBLOCKS, "qkv": QBLOCKS, "den": blocks_of(NT), "recT": TBLOCKS, "attn": OBLOCKS, "xn2T": TBLOCKS,
        "ff1": [(half, ts, c) for half, ts in TBLOCKS for c in range(2)], "ff2": OBLOCKS,
        "h1T": TBLOCKS, "z1": TBLOCKS, "out": OBLOCKS}
ORDER = [("xnT", 0, "AV"), ("qkv", 0, "AV"), ("xnT", 1, "AV"), ("qkv", 1, "AV"),
         ("den", 0, "V"), ("den", 1, "V"), ("recT", 0, "V"), ("recT", 1, "V"), ("attn", 0, "V"), ("attn", 1, "V"),
         ("xn2T", 0, "A"), ("ff1", 0, "AV"), ("xn2T", 1, "AV"), ("ff2", 0, "V"), ("ff1", 1, "A"), ("ff2", 1, "V"),
         ("h1T", 0, "AV"), ("h1T", 1, "AV"),
         ("z1", 0, "AV"), ("z1", 1, "AV"), ("out", 0, "V"), ("out", 1, "V")]


def number_jobs():
    table, n, emptied = {}, 0, {"A": 0, "V": 0}
    for name, half, engines in ORDER:
        for k in [k for k, job in enumerate(JOBS[name]) if job[0] == half]:
            engine = engines[k % len(engines)]
            emptied[engine] += 1
            table[name, k] = (n, emptied["A"], emptied["V"], engine)
            n += 1
    return table


NUMBERS = number_jobs()
BY_NUMBER = {v[0]: v for v in NUMBERS.values()}


def jobs_of(name, half, engine="AV"):
    return [(k, job[1:]) for k, job in enumerate(JOBS[name]) if job[0] == half and NUMBERS[name, k][3] in engine]


def last_of(name, half):
    return NUMBERS[name, jobs_of(name, half)[-1][0]]


PIECES = [HALVES[0], range(13, 19), range(19, NT)]


def build(nc, x, srcg, dstT, dstrow, eaT, wqkv, wo, ff1w, ff1b, ff2w, weT, w1T, w2T, cols, rows,
          q_table, kv_table, h_table, rel_table, out):
    with ExitStack() as ctx:
        def sb(name, shape, dt=F32):
            return ctx.enter_context(nc.sbuf_tensor(name, shape, dt))

        def psum(name, shape):
            return ctx.enter_context(nc.psum_tensor(name, shape, F32))

        def sem(name):
            return ctx.enter_context(nc.semaphore(name))

        iota_w = sb("iota_w", [P, P])
        iota_p = sb("iota_p", [P, 1])
        ident = sb("ident", [P, P])
        eps_col = sb("eps_col", [P, 1])
        zeros = sb("zeros", [P, D])
        wqkv_sb = sb("wqkv_sb", [D, 3 * D])
        wo_sb = sb("wo_sb", [D, D])
        ff1w_sb = sb("ff1w_sb", [D, FF])
        ff2w_sb = sb("ff2w_sb", [P, 2, D])
        weT_sb = sb("weT_sb", [EC + 1, D])
        w1T_sb = sb("w1T_sb", [D, D])
        w2T_sb = sb("w2T_sb", [D, D])
        cols_sb = sb("cols_sb", [D, 5])
        ff1b_sb = sb("ff1b_sb", [P, 2])
        rows_sb = sb("rows_sb", [P, 2, D])
        dstT_i = sb("dstT_i", [P, TILES], I32)
        base_i = sb("base_i", [P, TILES], I32)
        rel = sb("rel", [P, TILES])
        dst_rows = sb("dst_rows", [GROUPS, G, P], I32)
        rel_rows = sb("rel_rows", [GROUPS, G, P], BF16)
        minus_p = sb("minus_p", [P, 1])
        x_sb = sb("x_sb", [NP, NT, D])
        h_sb = sb("h_sb", [NP, NT, D])
        cen = sb("cen", [NP, NT, D])
        q_sb = sb("q_sb", [NP, NT, D])
        sq = q_sb
        rec_wide = cen
        kv_sb = sb("kv_sb", [NP, NT, 2 * D])
        x1_sb = sb("x1_sb", [NP, NT, D])
        stat = sb("stat", [NP, 5, NT])
        xnT = sb("xnT", [D, N])
        acc = sb("acc", [P, ACC_COLS])
        mT = sb("mT", [D, N])
        set_scratch = sb("set_scratch", [P, 1])
        rec = sb("rec", [NP, NT, H])
        ffT = sb("ffT", [P, 2, N])
        idx = [sb(f"idx{b}", [P, G], I32) for b in range(RING)]
        away = [sb(f"away{b}", [P, G * P], BF16) for b in range(2)]
        kv = [sb(f"kv{b}", [P, G, 2 * D]) for b in range(RING)]
        qwin = [sb(f"qwin{b}", [P, G, D]) for b in range(RING)]
        drow = [sb(f"drow{b}", [P, G * P], BF16) for b in range(RING)]
        ea = [sb(f"ea{b}", [EC + 1, G, P]) for b in range(RING)]
        spread = [sb(f"spread{b}", [P, G, P]) for b in range(2)]
        collect = [sb(f"collect{b}", [P, G, P]) for b in range(2)]
        prod = [sb(f"prod{b}", [P, G, D]) for b in range(2)]
        alpha = [sb(f"alpha{b}", [P, G * H]) for b in range(2)]
        vals = [sb(f"vals{b}", [P, G, VD]) for b in range(2)]

        ps_edge = [psum(f"ps_edge{b}", [P, 512]) for b in range(2)]
        ps_sum = [psum(f"ps_sum{b}", [P, G * P]) for b in range(2)]
        ps_node = [psum(f"ps_node{b}", [P, 512]) for b in range(2)]
        banks = [t[:, :] for t in ps_node + ps_edge] + [t[:, a:a + 512] for t in ps_sum for a in (0, 512)]
        positions = ps_node[0][:, 0:P]
        weights = ps_node[1][:, 0:G * H]

        x_landed = [sem(f"x_landed{half}") for half in range(2)]
        weights_landed = sem("weights_landed")
        dst_landed = sem("dst_landed")
        dst_rows_landed = sem("dst_rows_landed")
        rel_stored = sem("rel_stored")
        rel_made = sem("rel_made")
        tables_stored = sem("tables_stored")
        h_stored = sem("h_stored")
        out_stored = sem("out_stored")
        idx_landed = [sem(f"idx_landed{b}") for b in range(RING)]
        kv_landed = [sem(f"kv_landed{b}") for b in range(RING)]
        qwin_landed = [sem(f"qwin_landed{b}") for b in range(RING)]
        drow_landed = [sem(f"drow_landed{b}") for b in range(RING)]
        ea_landed = [sem(f"ea_landed{b}") for b in range(RING)]
        hg_landed = [sem(f"hg_landed{b}") for b in range(RING)]
        loads_begun = sem("loads_begun")
        gathers_begun = sem("gathers_begun")
        iotas_made = sem("iotas_made")
        consts_made = sem("consts_made")
        windows_made = sem("windows_made")
        acc_cleared = sem("acc_cleared")
        dve_chain = sem("dve_chain")
        variance_ready = sem("variance_ready")
        deviation_ready = sem("deviation_ready")
        normed = sem("normed")
        bank_filled = sem("bank_filled")
        emptied_act = sem("emptied_act")
        emptied_dve = sem("emptied_dve")
        centred = sem("centred")
        b2_added = sem("b2_added")
        rec_widened = sem("rec_widened")
        squared = sem("squared")
        x_biased = sem("x_biased")
        residual_made = sem("residual_made")
        away_made = sem("away_made")
        spread_made = sem("spread_made")
        spread_used = sem("spread_used")
        collect_made = sem("collect_made")
        prod_made = sem("prod_made")
        alpha_made = sem("alpha_made")
        exp_made = sem("exp_made")
        weights_made = sem("weights_made")
        vals_made = sem("vals_made")
        summed = sem("summed")
        added = sem("added")
        emb_made = sem("emb_made")
        collect1_made = sem("collect1_made")
        message_made = sem("message_made")
        relu_made = sem("relu_made")
        summed1 = sem("summed1")
        added1 = sem("added1")

        def rounds(engine, body):
            body(0, True, False)
            with engine.Fori(1, ROUNDS - 1) as r:
                body(r, False, False)
            body(ROUNDS - 1, False, True)

        def by_nodes(engine, dst_rows, src_rows, signal, partitions=(0, 112, NP)):
            for a, b in zip(partitions, partitions[1:]):
                engine.dma_start(dst_rows[a:b], src_rows[a:b]).then_inc(signal, 16)

        def dram_nodes(table, ts):
            return table[0:N, :].rearrange("(p t) d -> p t d", t=NT)[:, ts.start:ts.stop, :]

        def sbuf_nodes(tensor, ts):
            return tensor[:, ts.start:ts.stop, :]

        def by_columns_of(tensor, ts):
            return tensor[0:D, 0:N].rearrange("d (p t) -> d t p", t=NT)[:, ts.start:ts.stop, :]

        def as_columns(bank, ts):
            return bank[0:D, 0:len(ts) * NP].rearrange("d (t p) -> d t p", p=NP)

        def halves_done(half):
            return half + 1

        block = ctx.enter_context(nc.Block())

        @block.sync
        def _(sp):
            for half, ts in enumerate(HALVES):
                by_nodes(sp, sbuf_nodes(x_sb, ts), dram_nodes(x, ts), x_landed[half])
            sp.dma_start(dst_rows[:, :, :], dstrow[:, :, :]).then_inc(dst_rows_landed, 16)
            sp.dma_start(dstT_i[:, :], dstT[:, :]).then_inc(dst_landed, 16)
            sp.dma_start(base_i[:, :], dstT[0:1, :].partition_broadcast(P)).then_inc(dst_landed, 16)
            for b in range(RING):
                sp.dma_start(idx[b][:, :], srcg[b]).then_inc(idx_landed[b], 16)
                sp.dma_start(ea[b][:, :, :], eaT[b]).then_inc(ea_landed[b], 16)

            sp.wait_ge(rel_made, 1)
            sp.dma_start(rel_table[:, :], rel_rows[:, :, :].rearrange("g j e -> g (j e)")).then_inc(rel_stored, 16)
            sp.wait_ge(rel_stored, 16)
            for b in range(RING):
                sp.dma_start(drow[b][:, :], rel_table[b:b + 1, :].partition_broadcast(P)).then_inc(drow_landed[b], 16)

            sp.wait_ge(consts_made, 1)
            sp.dma_start(q_table[N:N + P, :], zeros[:, :]).then_inc(tables_stored, 16)
            for ts in PIECES:
                last_job = max(k for k, (_, us) in enumerate(QBLOCKS) if us.start < ts.stop)
                _, n_act, n_dve, _ = NUMBERS["qkv", last_job]
                sp.wait_ge(emptied_act, n_act)
                sp.wait_ge(emptied_dve, n_dve)
                by_nodes(sp, dram_nodes(q_table, ts), sbuf_nodes(q_sb, ts), tables_stored)
                by_nodes(sp, dram_nodes(kv_table, ts), sbuf_nodes(kv_sb, ts), tables_stored)

            def load_windows(group, b, slot_free):
                _, bases = nc.values_load_multi_w_load_instructions(
                    base_i[0:1, bass.ds(group * G, G)], engines=[ET.SP], min_val=0, max_val=N - 1,
                    skip_runtime_bounds_check_because="dst is a node's number, the first of a tile never padding")
                slot_free()
                for j in range(G):
                    sp.dma_start(qwin[b][:, j, :], q_table[bass.ds(bases[j], P), :]).then_inc(qwin_landed[b], 16)

            sp.wait_ge(tables_stored, 16 * TABLE_DMAS)
            sp.wait_ge(dst_landed, 32)
            for b in range(RING):
                load_windows(b, b, lambda: None)

            def next_inputs(r, first, last):
                if last:
                    return
                for b in range(RING):
                    group = r * RING + b
                    sp.wait_ge(kv_landed[b], 16 * G * (r + 1))
                    sp.dma_start(idx[b][:, :], srcg[bass.ds(group + RING, 1)].rearrange("a p j -> (a p) j")
                                 ).then_inc(idx_landed[b], 16)
                    sp.wait_ge(spread_made, group + 1)
                    sp.sem_inc(loads_begun, 1)
                    sp.dma_start(drow[b][:, :], rel_table[bass.ds(group + RING, 1), :].partition_broadcast(P)
                                 ).then_inc(drow_landed[b], 16)
                    load_windows(group + RING, b, lambda: sp.wait_ge(spread_used, group + 1))

            rounds(sp, next_inputs)

            for b in range(RING):
                sp.wait_ge(kv_landed[b], 16 * G * ROUNDS)
                sp.dma_start(idx[b][:, :], srcg[b]).then_inc(idx_landed[b], 16)

            for half, ts in enumerate(HALVES):
                sp.wait_ge(normed, 2 * 3 + halves_done(half))
                by_nodes(sp, dram_nodes(h_table, ts), sbuf_nodes(h_sb, ts), h_stored)

            def next_inputs1(r, first, last):
                if last:
                    return
                for b in range(RING):
                    group = r * RING + b
                    sp.wait_ge(hg_landed[b], 16 * G * (r + 1))
                    sp.dma_start(idx[b][:, :], srcg[bass.ds(group + RING, 1)].rearrange("a p j -> (a p) j")
                                 ).then_inc(idx_landed[b], 16)
                    sp.wait_ge(emb_made, group + 1)
                    sp.dma_start(ea[b][:, :, :], eaT[bass.ds(group + RING, 1)].rearrange("a c j e -> (a c) j e")
                                 ).then_inc(ea_landed[b], 16)

            rounds(sp, next_inputs1)

            for k, (_, ts) in enumerate(OBLOCKS):
                sp.wait_ge(emptied_dve, NUMBERS["out", k][2])
                by_nodes(sp, dram_nodes(out, ts), sbuf_nodes(h_sb, ts), out_stored)
            sp.wait_ge(out_stored, 32 * len(OBLOCKS))

        @block.gpsimd
        def _(pool):
            nc.gpsimd.iota(iota_w[:, :], [[1, P]], base=0, channel_multiplier=0,
                           allow_small_or_imprecise_dtypes=True).then_inc(iotas_made, 1)
            nc.gpsimd.iota(iota_p[:, :], [[0, 1]], base=0, channel_multiplier=1,
                           allow_small_or_imprecise_dtypes=True).then_inc(iotas_made, 1)

            def load(dst, src):
                pool.dma_start(dst, src).then_inc(weights_landed, 16)

            load(cols_sb[:, :], cols[:, :])
            load(wqkv_sb[:, :], wqkv[:, :])
            load(wo_sb[:, :], wo[:, :])
            load(ff1w_sb[:, :], ff1w[:, :])
            load(ff1b_sb[:, :], ff1b[:, :])
            load(ff2w_sb[:, :, :], ff2w[:, :].rearrange("(c p) n -> p c n", p=P))
            load(rows_sb[:, :, :], rows[:, :, :].partition_broadcast(P))
            load(weT_sb[:, :], weT[:, :])
            load(w1T_sb[:, :], w1T[:, :])
            load(w2T_sb[:, :], w2T[:, :])

            pool.wait_ge(iotas_made, 2)
            nc.gpsimd.memset(acc[0:D, :], 0.0).then_inc(acc_cleared, 1)
            pool.wait_ge(acc_cleared, 1)
            nc.gpsimd.memset(acc[D:VD, :], DEN_EPS).then_inc(acc_cleared, 1)
            pool.wait_ge(acc_cleared, 2)
            pool.wait_ge(weights_landed, 16 * WEIGHT_DMAS)
            for half, ts in enumerate(HALVES):
                pool.wait_ge(centred, halves_done(half))
                nc.gpsimd.tensor_tensor(sbuf_nodes(x_sb, ts), sbuf_nodes(x_sb, ts),
                                        rows_sb[0:NP, 0:1, :].to_broadcast([NP, len(ts), D]),
                                        ALU.add).then_inc(x_biased, 1)

            def gather(r, b, table, width, landed):
                for j in range(G):
                    pool.indirect_dma_start(
                        out=kv[b][:, j, 0:width], out_offset=None, in_=table,
                        in_offset=bass.IndirectOffsetOnAxis(ap=idx[b][:, j:j + 1], axis=0)).then_inc(landed[b], 16)

            def gather_kv(r, first, last):
                for b in range(RING):
                    pool.wait_ge(idx_landed[b], 16 * (r + 1))
                    if not first:
                        pool.wait_ge(vals_made, (r - 1) * RING + b + 1)
                    pool.sem_inc(gathers_begun, 1)
                    gather(r, b, kv_table[:, :], 2 * D, kv_landed)

            pool.wait_ge(tables_stored, 16 * TABLE_DMAS)
            rounds(pool, gather_kv)

            def gather_h(r, first, last):
                for b in range(RING):
                    pool.wait_ge(idx_landed[b], 16 * (ROUNDS + r + 1))
                    if not first:
                        pool.wait_ge(message_made, (r - 1) * RING + b + 1)
                    pool.sem_inc(gathers_begun, 1)
                    gather(r, b, h_table[:, :], D, hg_landed)

            pool.wait_ge(x_biased, 2)
            for half, ts in enumerate(HALVES):
                pool.wait_ge(centred, 2 * 2 + halves_done(half))
                nc.gpsimd.tensor_tensor(sbuf_nodes(x1_sb, ts), sbuf_nodes(x1_sb, ts), sbuf_nodes(x_sb, ts),
                                        ALU.add).then_inc(residual_made, 1)

            pool.wait_ge(h_stored, 64)
            rounds(pool, gather_h)

        @block.tensor
        def _(pe):
            def emptied(job):
                _, n_act, n_dve, _ = job
                if n_act:
                    pe.wait_ge(emptied_act, n_act)
                if n_dve:
                    pe.wait_ge(emptied_dve, n_dve)

            def bank_of(name, k):
                n = NUMBERS[name, k][0]
                if n >= len(banks):
                    emptied(BY_NUMBER[n - len(banks)])
                return banks[n % len(banks)]

            def transposes(name, half, source, norm):
                pe.wait_ge(normed, 2 * norm + halves_done(half))
                for k, (ts,) in jobs_of(name, half):
                    bank = bank_of(name, k)
                    for i, t in enumerate(ts):
                        last = nc.tensor.transpose(bank[0:D, i * NP:(i + 1) * NP], source[:, t, :],
                                                   ident[0:NP, 0:NP])
                    last.then_inc(bank_filled, 1)

            def by_columns(name, half, source, weights_sb, width):
                for k, (ts,) in jobs_of(name, half):
                    bank = bank_of(name, k)
                    for i, t in enumerate(ts):
                        last = nc.tensor.matmul(bank[0:NP, i * width:(i + 1) * width],
                                                source[:, t * NP:(t + 1) * NP], weights_sb[:, :],
                                                start=True, stop=True)
                    last.then_inc(bank_filled, 1)

            pe.wait_ge(consts_made, 1)
            pe.wait_ge(weights_landed, 16 * WEIGHT_DMAS)
            for half in range(2):
                transposes("xnT", half, cen, 1)
                emptied(last_of("xnT", half))
                by_columns("qkv", half, xnT, wqkv_sb, 3 * D)

            def expand(r, b, first):
                group = r * RING + b
                pe.wait_ge(spread_made, group + 1)
                pe.wait_ge(qwin_landed[b], 16 * G * (r + 1))
                if not (first and b < 2):
                    pe.wait_ge(prod_made, group - 1)
                for j in range(G):
                    last = nc.tensor.matmul(ps_edge[b % 2][:, j * D:(j + 1) * D], spread[b % 2][:, j, :],
                                            qwin[b][:, j, :], start=True, stop=True)
                last.then_inc(spread_used, 1)

            def edges0(r, first, last_round):
                if first:
                    expand(0, 0, True)
                for b in range(RING):
                    group = r * RING + b
                    if b + 1 < RING:
                        expand(r, b + 1, first)
                    elif not last_round:
                        expand(r + 1, 0, False)
                    pe.wait_ge(vals_made, group + 1)
                    pe.wait_ge(weights_made, group + 1)
                    pe.wait_ge(collect_made, group + 1)
                    if not (first and b < 2):
                        pe.wait_ge(added, G * (group - 1))
                    for j in range(G):
                        last = nc.tensor.matmul(ps_sum[b % 2][0:VD, j * P:(j + 1) * P], vals[b % 2][:, j, :],
                                                collect[b % 2][:, j, :], start=True, stop=True)
                    last.then_inc(summed, 1)

            emptied(last_of("qkv", 1))
            rounds(pe, edges0)

            pe.wait_ge(added, G * GROUPS)
            for half in range(2):
                for k, (ts,) in jobs_of("den", half):
                    bank = bank_of("den", k)
                    for i, t in enumerate(ts):
                        last = nc.tensor.matmul(bank[0:NP, i * H:(i + 1) * H], acc[D:VD, t:N:NT],
                                                ident[D:VD, D:VD], start=True, stop=True)
                    last.then_inc(bank_filled, 1)
            for half in range(2):
                pe.wait_ge(rec_widened, halves_done(half))
                for k, (ts,) in jobs_of("recT", half):
                    bank = bank_of("recT", k)
                    for i, t in enumerate(ts):
                        last = nc.tensor.transpose(bank[0:D, i * NP:(i + 1) * NP],
                                                   rec_wide[:, t, :],
                                                   ident[0:NP, 0:NP])
                    last.then_inc(bank_filled, 1)
            for half in range(2):
                emptied(last_of("recT", half))
                by_columns("attn", half, mT, wo_sb, D)

            def ff1(half):
                for k, (ts, c) in jobs_of("ff1", half):
                    bank = bank_of("ff1", k)
                    emptied(NUMBERS["xn2T", k // 2])
                    nc.tensor.matmul(bank[:, 0:len(ts) * NP], ff1w_sb[:, c * P:(c + 1) * P],
                                     xnT[:, ts.start * NP:ts.stop * NP], start=True, stop=True
                                     ).then_inc(bank_filled, 1)

            def ff2(half):
                emptied(last_of("ff1", half))
                for k, (ts,) in jobs_of("ff2", half):
                    bank = bank_of("ff2", k)
                    for i, t in enumerate(ts):
                        for c in range(2):
                            last = nc.tensor.matmul(bank[0:NP, i * D:(i + 1) * D], ffT[:, c, t * NP:(t + 1) * NP],
                                                    ff2w_sb[:, c, :], start=(c == 0), stop=(c == 1))
                    last.then_inc(bank_filled, 1)

            transposes("xn2T", 0, cen, 2)
            ff1(0)
            transposes("xn2T", 1, cen, 2)
            ff2(0)
            ff1(1)
            ff2(1)
            for half in range(2):
                transposes("h1T", half, h_sb, 3)

            def embed(r, b, first):
                group = r * RING + b
                pe.wait_ge(ea_landed[b], 16 * (r + 1))
                if not (first and b < 2):
                    pe.wait_ge(message_made, group - 1)
                for j in range(G):
                    last = nc.tensor.matmul(ps_edge[b % 2][:, j * D:(j + 1) * D], ea[b][:, j, :],
                                            weT_sb[:, :], start=True, stop=True)
                last.then_inc(emb_made, 1)

            def edges1(r, first, last_round):
                if first:
                    embed(0, 0, True)
                for b in range(RING):
                    group = r * RING + b
                    if b + 1 < RING:
                        embed(r, b + 1, first)
                    elif not last_round:
                        embed(r + 1, 0, False)
                    pe.wait_ge(relu_made, group + 1)
                    pe.wait_ge(collect1_made, group + 1)
                    if not (first and b < 2):
                        pe.wait_ge(added1, G * (group - 1))
                    for j in range(G):
                        last = nc.tensor.matmul(ps_sum[b % 2][0:D, j * P:(j + 1) * P], vals[b % 2][:, j, 0:D],
                                                collect[b % 2][:, j, :], start=True, stop=True)
                    last.then_inc(summed1, 1)

            emptied(last_of("h1T", 1))
            rounds(pe, edges1)

            pe.wait_ge(added1, G * GROUPS)
            for half in range(2):
                for k, (ts,) in jobs_of("z1", half):
                    bank = bank_of("z1", k)
                    nc.tensor.matmul(bank[0:D, 0:len(ts) * NP], w1T_sb[:, :],
                                     by_columns_of(acc, ts), start=True, stop=True).then_inc(bank_filled, 1)
            for half in range(2):
                emptied(last_of("z1", half))
                by_columns("out", half, mT, w2T_sb, D)

        @block.scalar
        def _(act):
            def squares(n, half):
                ts = HALVES[half]
                act.wait_ge(centred, 2 * n + halves_done(half))
                nc.scalar.activation(sbuf_nodes(sq, ts), sbuf_nodes(cen, ts), ACT.Square).then_inc(squared, 1)

            def deviations(n, half):
                ts = HALVES[half]
                act.wait_ge(variance_ready, 2 * n + halves_done(half))
                nc.scalar.activation(stat[:, 3, ts.start:ts.stop], stat[:, 2, ts.start:ts.stop], ACT.Sqrt,
                                     bias=eps_col[0:NP, :], scale=1.0 / D).then_inc(deviation_ready, 1)

            def fetch_sqrt():
                nc.scalar.activation(set_scratch[:, :], eps_col[:, :], ACT.Sqrt)

            def filled(name, k):
                n = NUMBERS[name, k][0]
                act.wait_ge(bank_filled, n + 1)
                return banks[n % len(banks)]

            def scaled_transpose(name, k, ts, g, b):
                bank = filled(name, k)
                nc.scalar.activation(xnT[:, ts.start * NP:ts.stop * NP], bank[0:D, 0:len(ts) * NP],
                                     ACT.Identity, bias=cols_sb[:, b:b + 1], scale=cols_sb[:, g:g + 1]
                                     ).then_inc(emptied_act, 1)

            act.wait_ge(consts_made, 1)
            fetch_sqrt()
            squares(0, 0)
            squares(0, 1)
            deviations(0, 0)
            deviations(0, 1)
            squares(1, 0)
            deviations(1, 0)
            squares(1, 1)
            deviations(1, 1)
            act.wait_ge(weights_landed, 16 * WEIGHT_DMAS)
            for half in range(2):
                for k, (ts,) in jobs_of("xnT", half, "A"):
                    scaled_transpose("xnT", k, ts, 0, 1)
                for k, (ts,) in jobs_of("qkv", half, "A"):
                    bank = filled("qkv", k)
                    view = bank[0:NP, 0:len(ts) * 3 * D].rearrange("p (t c) -> p t c", c=3 * D)
                    nc.scalar.activation(sbuf_nodes(q_sb, ts), view[:, :, 0:D], ACT.Copy, scale=HD ** -0.5)
                    nc.scalar.activation(sbuf_nodes(kv_sb, ts), view[:, :, D:3 * D], ACT.Copy
                                         ).then_inc(emptied_act, 1)

            def make_spread(r, b, first):
                group = r * RING + b
                act.wait_ge(drow_landed[b], 16 * (r + 1))
                nc.scalar.activation(away[b % 2][:, :], drow[b][:, :], ACT.Abs,
                                     bias=minus_p[:, :]).then_inc(away_made, 1)
                if not (first and b < 2):
                    act.wait_ge(spread_used, group - 1)
                act.wait_ge(away_made, group + 1)
                nc.scalar.activation(spread[b % 2][:, :, :].rearrange("p j e -> p (j e)"), away[b % 2][:, :], ACT.Relu,
                                     bias=1.0, scale=-1.0).then_inc(spread_made, 1)

            def exps(r, first, last):
                if first:
                    make_spread(0, 0, True)
                for b in range(RING):
                    group = r * RING + b
                    if b + 1 < RING:
                        make_spread(r, b + 1, first)
                    elif not last:
                        make_spread(r + 1, 0, False)
                    act.wait_ge(alpha_made, group + 1)
                    if not (first and b == 0):
                        act.wait_ge(vals_made, group)
                    nc.scalar.activation(weights, alpha[b % 2][:, :], ACT.Exp).then_inc(exp_made, 1)
                    if not (first and b < 2):
                        act.wait_ge(summed, group - 1)
                    nc.scalar.activation(vals[b % 2][:, :, D:VD],
                                         alpha[b % 2][:, :].rearrange("p (j h) -> p j h", h=H),
                                         ACT.Exp).then_inc(weights_made, 1)

            act.wait_ge(emptied_act, last_of("qkv", 1)[1])
            act.wait_ge(emptied_dve, last_of("qkv", 1)[2])
            rounds(act, exps)

            def relu_of(k, ts, c):
                bank = filled("ff1", k)
                nc.scalar.activation(ffT[:, c, ts.start * NP:ts.stop * NP], bank[:, 0:len(ts) * NP], ACT.Relu,
                                     bias=ff1b_sb[:, c:c + 1]).then_inc(emptied_act, 1)

            fetch_sqrt()
            for half, ts in enumerate(HALVES):
                act.wait_ge(emptied_dve, last_of("den", half)[2])
                nc.scalar.activation(sbuf_nodes(rec_wide, ts).rearrange("p t (h c) -> p t h c", c=HD),
                                     sbuf_nodes(rec, ts).unsqueeze(3).to_broadcast([NP, len(ts), H, HD]),
                                     ACT.Copy).then_inc(rec_widened, 1)
            squares(2, 0)
            deviations(2, 0)
            for step, (k, (ts,)) in enumerate(jobs_of("xn2T", 0, "A")):
                if step == 1:
                    squares(2, 1)
                if step == 3:
                    deviations(2, 1)
                scaled_transpose("xn2T", k, ts, 2, 3)
            for k, (ts, c) in jobs_of("ff1", 0, "A"):
                relu_of(k, ts, c)
            for k, (ts,) in jobs_of("xn2T", 1, "A"):
                scaled_transpose("xn2T", k, ts, 2, 3)
            for step, (k, (ts, c)) in enumerate(jobs_of("ff1", 1, "A")):
                if step == 3:
                    squares(3, 0)
                if step == 5:
                    deviations(3, 0)
                relu_of(k, ts, c)
            squares(3, 1)
            deviations(3, 1)
            for half in range(2):
                for k, (ts,) in jobs_of("h1T", half, "A"):
                    bank = filled("h1T", k)
                    nc.scalar.activation(by_columns_of(acc, ts), as_columns(bank, ts), ACT.Copy
                                         ).then_inc(emptied_act, 1)

            def relus(r, first, last):
                for b in range(RING):
                    group = r * RING + b
                    act.wait_ge(message_made, group + 1)
                    if not (first and b < 2):
                        act.wait_ge(summed1, group - 1)
                    nc.scalar.activation(vals[b % 2][:, :, 0:D], prod[b % 2][:, :, :],
                                         ACT.Relu).then_inc(relu_made, 1)

            rounds(act, relus)

            for half in range(2):
                for k, (ts,) in jobs_of("z1", half, "A"):
                    bank = filled("z1", k)
                    nc.scalar.activation(mT[:, ts.start * NP:ts.stop * NP], bank[0:D, 0:len(ts) * NP], ACT.Relu,
                                         bias=cols_sb[:, 4:5]).then_inc(emptied_act, 1)

        @block.vector
        def _(dve):
            done = [0]

            def link(ins):
                done[0] += 1
                ins.then_inc(dve_chain, 1)
                dve.wait_ge(dve_chain, done[0])

            nc.vector.memset(eps_col[:, :], EPS)
            nc.vector.memset(zeros[:, :], 0.0)
            dve.wait_ge(iotas_made, 2)
            nc.vector.tensor_scalar(minus_p[:, :], iota_p[:, :], -1.0, None, ALU.mult)
            nc.vector.tensor_tensor(ident[:, :], iota_w[:, :], iota_p[:, 0:1].to_broadcast([P, P]),
                                    ALU.is_equal).then_inc(consts_made, 1)

            def over_features(column, ts):
                return stat[:, column, ts.start:ts.stop].unsqueeze(2).to_broadcast([NP, len(ts), D])

            def norm_centre(half, source):
                ts = HALVES[half]
                link(nc.vector.tensor_reduce(stat[:, 0, ts.start:ts.stop], sbuf_nodes(source, ts), AX.X, ALU.add))
                nc.vector.scalar_tensor_tensor(sbuf_nodes(cen, ts), over_features(0, ts), -1.0 / D,
                                               sbuf_nodes(source, ts), ALU.mult, ALU.add).then_inc(centred, 1)

            def norm_variance(n, half):
                ts = HALVES[half]
                dve.wait_ge(squared, 2 * n + halves_done(half))
                nc.vector.tensor_reduce(stat[:, 2, ts.start:ts.stop], sbuf_nodes(sq, ts), AX.X,
                                        ALU.add).then_inc(variance_ready, 1)

            def norm_scale(n, half, result, op0, scalar):
                ts = HALVES[half]
                dve.wait_ge(deviation_ready, 2 * n + halves_done(half))
                link(nc.vector.reciprocal(stat[:, 4, ts.start:ts.stop], stat[:, 3, ts.start:ts.stop]))
                nc.vector.scalar_tensor_tensor(sbuf_nodes(result, ts), sbuf_nodes(cen, ts), scalar,
                                               over_features(4, ts), op0, ALU.mult).then_inc(normed, 1)

            def filled(name, k):
                n = NUMBERS[name, k][0]
                dve.wait_ge(bank_filled, n + 1)
                return banks[n % len(banks)]

            dve.wait_ge(dst_rows_landed, 16)
            nc.vector.tensor_tensor(rel_rows[:, :, :], dst_rows[:, :, :],
                                    dst_rows[:, :, 0:1].to_broadcast([GROUPS, G, P]), ALU.subtract
                                    ).then_inc(rel_made, 1)
            dve.wait_ge(x_landed[0], 32)
            norm_centre(0, x_sb)
            dve.wait_ge(x_landed[1], 32)
            norm_centre(1, x_sb)
            norm_variance(0, 0)
            norm_variance(0, 1)
            norm_scale(0, 0, h_sb, ALU.max, 0.0)
            dve.wait_ge(normed, 1)
            norm_centre(0, h_sb)
            norm_scale(0, 1, h_sb, ALU.max, 0.0)
            norm_variance(1, 0)
            dve.wait_ge(normed, 2)
            norm_centre(1, h_sb)
            norm_scale(1, 0, cen, ALU.mult, 1.0)
            norm_variance(1, 1)
            norm_scale(1, 1, cen, ALU.mult, 1.0)

            dve.wait_ge(dst_landed, 32)
            nc.vector.tensor_tensor(rel[:, :], dstT_i[:, :], base_i[:, :], ALU.subtract).then_inc(windows_made, 1)
            dve.wait_ge(weights_landed, 16 * WEIGHT_DMAS)

            def scaled_transposes(name, half, g, b):
                for k, (ts,) in jobs_of(name, half, "V"):
                    bank = filled(name, k)
                    nc.vector.tensor_scalar(xnT[:, ts.start * NP:ts.stop * NP], bank[0:D, 0:len(ts) * NP],
                                            cols_sb[:, g:g + 1], cols_sb[:, b:b + 1], ALU.mult, ALU.add
                                            ).then_inc(emptied_dve, 1)

            for half in range(2):
                scaled_transposes("xnT", half, 0, 1)
                for k, (ts,) in jobs_of("qkv", half, "V"):
                    bank = filled("qkv", k)
                    view = bank[0:NP, 0:len(ts) * 3 * D].rearrange("p (t c) -> p t c", c=3 * D)
                    nc.vector.tensor_scalar(sbuf_nodes(q_sb, ts), view[:, :, 0:D], HD ** -0.5, None, ALU.mult)
                    nc.vector.tensor_copy(sbuf_nodes(kv_sb, ts), view[:, :, D:3 * D]).then_inc(emptied_dve, 1)

            dve.wait_ge(emptied_act, last_of("qkv", 1)[1])
            dve.wait_ge(emptied_dve, last_of("qkv", 1)[2])
            dve.wait_ge(windows_made, 1)
            link(nc.vector.tensor_copy(positions, iota_w[:, :]))

            def make_collect(r, b, first, used, made):
                group = r * RING + b
                if not (first and b < 2):
                    dve.wait_ge(used, group - 1)
                nc.vector.tensor_tensor(collect[b % 2][:, :, :],
                                        positions.unsqueeze(1).to_broadcast([P, G, P]),
                                        rel[:, bass.ds(group * G, G)].unsqueeze(2).to_broadcast([P, G, P]),
                                        ALU.is_equal).then_inc(made, 1)

            def add_windows(group, b, rows, was_summed, was_added, none_before):
                _, bases = nc.values_load_multi_w_load_instructions(
                    base_i[0:1, bass.ds(group * G, G)], engines=[ET.DVE], min_val=0, max_val=N - 1,
                    skip_runtime_bounds_check_because="dst is a node's number, the first of a tile never padding")
                dve.wait_ge(was_summed, group + 1)
                for j in range(G):
                    if not (none_before and j == 0):
                        dve.wait_ge(was_added, group * G + j)
                    window = acc[0:rows, bass.ds(bases[j], P)]
                    nc.vector.tensor_tensor(window, window, ps_sum[b % 2][0:rows, j * P:(j + 1) * P],
                                            ALU.add).then_inc(was_added, 1)

            def edges0(r, first, last_round):
                for b in range(RING):
                    group = r * RING + b
                    make_collect(r, b, first, summed, collect_made)
                    dve.wait_ge(kv_landed[b], 16 * G * (r + 1))
                    dve.wait_ge(spread_used, group + 1)
                    nc.vector.tensor_tensor(prod[b % 2][:, :, :],
                                            ps_edge[b % 2][:, :].rearrange("p (j c) -> p j c", c=D),
                                            kv[b][:, :, 0:D], ALU.mult).then_inc(prod_made, 1)
                    dve.wait_ge(prod_made, group + 1)
                    if not (first and b < 2):
                        dve.wait_ge(weights_made, group - 1)
                    nc.vector.tensor_reduce(alpha[b % 2][:, :],
                                            prod[b % 2][:, :, :].rearrange("p j (h c) -> p (j h) c", c=HD),
                                            AX.X, ALU.add).then_inc(alpha_made, 1)
                    last_group = last_round and b == RING - 1
                    if not (first and b == 0 or last_group):
                        add_windows(group - 1, (b - 1) % 2, VD, summed, added, first and b == 1)
                    dve.wait_ge(exp_made, group + 1)
                    if not (first and b < 2):
                        dve.wait_ge(summed, group - 1)
                    nc.vector.tensor_tensor(vals[b % 2][:, :, 0:D].rearrange("p j (h c) -> p j h c", c=HD),
                                            kv[b][:, :, D:2 * D].rearrange("p j (h c) -> p j h c", c=HD),
                                            weights.rearrange("p (j h) -> p j h", h=H).unsqueeze(3)
                                            .to_broadcast([P, G, H, HD]),
                                            ALU.mult).then_inc(vals_made, 1)
                    if last_group:
                        add_windows(group - 1, (b - 1) % 2, VD, summed, added, False)

            dve.wait_ge(acc_cleared, 2)
            rounds(dve, edges0)
            add_windows(GROUPS - 1, (RING - 1) % 2, VD, summed, added, False)

            for half in range(2):
                for k, (ts,) in jobs_of("den", half, "V"):
                    bank = filled("den", k)
                    nc.vector.reciprocal(sbuf_nodes(rec, ts),
                                         bank[0:NP, 0:len(ts) * H].rearrange("p (t h) -> p t h", h=H)
                                         ).then_inc(emptied_dve, 1)
            dve.wait_ge(added, G * GROUPS)
            for half in range(2):
                for k, (ts,) in jobs_of("recT", half, "V"):
                    bank = filled("recT", k)
                    nc.vector.tensor_tensor(mT[:, ts.start * NP:ts.stop * NP].rearrange("d (t p) -> d t p", p=NP),
                                            by_columns_of(acc, ts), as_columns(bank, ts),
                                            ALU.mult).then_inc(emptied_dve, 1)

            def add_banks(name, half, result, other):
                for k, (ts,) in jobs_of(name, half, "V"):
                    bank = filled(name, k)
                    nc.vector.tensor_tensor(sbuf_nodes(result, ts),
                                            bank[0:NP, 0:len(ts) * D].rearrange("p (t d) -> p t d", d=D),
                                            sbuf_nodes(other, ts), ALU.add).then_inc(emptied_dve, 1)

            def relus_of(half):
                for k, (ts, c) in jobs_of("ff1", half, "V"):
                    bank = filled("ff1", k)
                    nc.vector.tensor_scalar(ffT[:, c, ts.start * NP:ts.stop * NP], bank[:, 0:len(ts) * NP],
                                            ff1b_sb[:, c:c + 1], 0.0, ALU.add, ALU.max).then_inc(emptied_dve, 1)

            add_banks("attn", 0, x1_sb, h_sb)
            dve.wait_ge(emptied_dve, last_of("attn", 0)[2])
            norm_centre(0, x1_sb)
            norm_variance(2, 0)
            add_banks("attn", 1, x1_sb, h_sb)
            norm_scale(2, 0, cen, ALU.mult, 1.0)
            dve.wait_ge(emptied_dve, last_of("attn", 1)[2])
            norm_centre(1, x1_sb)
            norm_variance(2, 1)
            norm_scale(2, 1, cen, ALU.mult, 1.0)

            relus_of(0)
            scaled_transposes("xn2T", 1, 2, 3)
            relus_of(1)
            dve.wait_ge(residual_made, 1)
            add_banks("ff2", 0, x_sb, x1_sb)
            dve.wait_ge(emptied_dve, last_of("ff2", 0)[2])
            norm_centre(0, x_sb)
            norm_variance(3, 0)
            norm_scale(3, 0, h_sb, ALU.max, 0.0)
            dve.wait_ge(residual_made, 2)
            add_banks("ff2", 1, x_sb, x1_sb)
            dve.wait_ge(emptied_dve, last_of("ff2", 1)[2])
            norm_centre(1, x_sb)
            norm_variance(3, 1)
            norm_scale(3, 1, h_sb, ALU.max, 0.0)
            for half in range(2):
                for k, (ts,) in jobs_of("h1T", half, "V"):
                    bank = filled("h1T", k)
                    nc.vector.tensor_copy(by_columns_of(acc, ts), as_columns(bank, ts)).then_inc(emptied_dve, 1)
            dve.wait_ge(centred, 8)
            nc.vector.tensor_tensor(x_sb[:, :, :], x_sb[:, :, :], rows_sb[0:NP, 1:2, :].to_broadcast([NP, NT, D]),
                                    ALU.add).then_inc(b2_added, 1)

            dve.wait_ge(emptied_act, last_of("h1T", 1)[1])
            dve.wait_ge(emptied_dve, last_of("h1T", 1)[2])
            link(nc.vector.tensor_copy(positions, iota_w[:, :]))

            def edges1(r, first, last_round):
                for b in range(RING):
                    group = r * RING + b
                    make_collect(r, b, first, summed1, collect1_made)
                    dve.wait_ge(hg_landed[b], 16 * G * (r + 1))
                    dve.wait_ge(emb_made, group + 1)
                    if not (first and b < 2):
                        dve.wait_ge(relu_made, group - 1)
                    nc.vector.tensor_tensor(prod[b % 2][:, :, :],
                                            ps_edge[b % 2][:, :].rearrange("p (j c) -> p j c", c=D),
                                            kv[b][:, :, 0:D], ALU.add).then_inc(message_made, 1)
                    if not (first and b == 0):
                        add_windows(group - 1, (b - 1) % 2, D, summed1, added1, first and b == 1)

            rounds(dve, edges1)
            add_windows(GROUPS - 1, (RING - 1) % 2, D, summed1, added1, False)

            for half in range(2):
                for k, (ts,) in jobs_of("z1", half, "V"):
                    bank = filled("z1", k)
                    nc.vector.tensor_scalar(mT[:, ts.start * NP:ts.stop * NP], bank[0:D, 0:len(ts) * NP],
                                            cols_sb[:, 4:5], 0.0, ALU.add, ALU.max).then_inc(emptied_dve, 1)
            dve.wait_ge(b2_added, 1)
            for half in range(2):
                add_banks("out", half, h_sb, x_sb)


WEIGHT_DMAS = 10
TABLE_DMAS = 1 + 4 * len(PIECES)


def kernel(**inputs):
    import numpy as _np
    import concourse.bacc as _bacc
    from concourse import mybir as _mybir
    from concourse.bass_utils import run_bass_kernel_spmd as _run

    a = {k: _np.asarray(v) for k, v in inputs.items()}
    edges = TILES * P

    def padded(v, fill):
        return _np.concatenate([v, _np.full((edges - E,) + v.shape[1:], fill, v.dtype)])

    src, dst = padded(a["src"], 0), padded(a["dst"], -1)
    edge_attr = padded(a["edge_attr_32"], 0)
    wqkv = _np.concatenate([a["L0_gnn_w_q"], a["L0_gnn_w_k"], a["L0_gnn_w_v"]], axis=1)
    laid = {
        "x": a["x"],
        "srcg": src.reshape(GROUPS, G, P).transpose(0, 2, 1),
        "dstT": dst.reshape(TILES, P).T,
        "dstrow": dst.reshape(GROUPS, G, P),
        "eaT": _np.concatenate([edge_attr.reshape(GROUPS, G, P, EC).transpose(0, 3, 1, 2),
                                _np.ones((GROUPS, 1, G, P), edge_attr.dtype)], axis=1),
        "wqkv": wqkv,
        "wo": a["L0_gnn_w_o"],
        "ff1w": a["L0_gnn_ff1_w"], "ff1b": a["L0_gnn_ff1_b"].reshape(2, P).T, "ff2w": a["L0_gnn_ff2_w"],
        "weT": _np.concatenate([a["L1_gnn_We"].T, a["L1_gnn_be"][None]]),
        "w1T": a["L1_gnn_W1"].T, "w2T": a["L1_gnn_W2"].T,
        "cols": _np.stack([a["L0_gnn_ln1_g"], a["L0_gnn_ln1_b"], a["L0_gnn_ln2_g"], a["L0_gnn_ln2_b"],
                           a["L1_gnn_b1"]], axis=1),
        "rows": _np.stack([a["L0_gnn_ff2_b"], a["L1_gnn_b2"]])[None],
    }
    nc = _bacc.Bacc("TRN2", target_bir_lowering=False, num_devices=1)
    arrays, args = {}, []
    for name, v in laid.items():
        v = _np.ascontiguousarray(v)
        arrays[f"in_{name}"] = v
        args.append(nc.dram_tensor(f"in_{name}", v.shape, _mybir.dt.from_np(v.dtype), kind="ExternalInput").ap())
    f32 = _mybir.dt.float32
    tables = [nc.dram_tensor("q_table", (ACC_COLS, D), f32, kind="Internal").ap(),
              nc.dram_tensor("kv_table", (N, 2 * D), f32, kind="Internal").ap(),
              nc.dram_tensor("h_table", (N, D), f32, kind="Internal").ap(),
              nc.dram_tensor("rel_table", (GROUPS, G * P), _mybir.dt.bfloat16, kind="Internal").ap()]
    out = nc.dram_tensor("out_0", (N, D), f32, kind="ExternalOutput").ap()
    build(nc, *args, *tables, out)
    r = _run(nc, [arrays], core_ids=[0])
    return r.results[0]["out_0"]
```

```python
from contextlib import ExitStack

import concourse.bass as bass
from concourse import mybir

F32 = mybir.dt.float32
BF16 = mybir.dt.bfloat16
I32 = mybir.dt.int32
ALU = mybir.AluOpType
ACT = mybir.ActivationFunctionType
AX = mybir.AxisListType
ET = mybir.EngineType

N, D, H, FF, EC = 3125, 64, 4, 256, 32
E = 53125
HD = D // H
P = 128
NP, NT = 125, 25
TILES = -(-E // P)
G = 4
GROUPS = TILES // G
RING = 8
ROUNDS = GROUPS // RING
ACC_COLS = N + P
VD = D + H
EPS = 1e-5
DEN_EPS = 1e-16
WARM_UPS = {"xnT": 2, "last sums": 1, "den": 1, "recT": 1, "xn2T": 2, "last sums 1": 1, "z1": 1}
assert TILES % G == 0 and GROUPS % RING == 0 and NP * NT == N

HALVES = [range(0, 13), range(13, NT)]


def blocks_of(size):
    return [(half, range(a, min(a + size, ts.stop))) for half, ts in enumerate(HALVES)
            for a in range(ts.start, ts.stop, size)]


TBLOCKS = blocks_of(4)
QBLOCKS = blocks_of(2)
JOBS = {"xnT": TBLOCKS, "qkv": QBLOCKS, "den": blocks_of(NT), "recT": TBLOCKS, "attn": TBLOCKS, "xn2T": TBLOCKS,
        "ff1": [(half, ts, c) for half, ts in TBLOCKS for c in range(2)], "ff2": TBLOCKS,
        "h1T": TBLOCKS, "z1": TBLOCKS, "out": TBLOCKS}
ORDER = [("xnT", 0, "AV"), ("qkv", 0, "AV"), ("xnT", 1, "AV"), ("qkv", 1, "AV"),
         ("den", 0, "V"), ("den", 1, "V"), ("recT", 0, "V"), ("recT", 1, "V"), ("attn", 0, "V"), ("attn", 1, "V"),
         ("xn2T", 0, "A"), ("ff1", 0, "AV"), ("xn2T", 1, "AV"), ("ff2", 0, "V"), ("ff1", 1, "A"), ("ff2", 1, "V"),
         ("h1T", 0, "AV"), ("h1T", 1, "AV"),
         ("z1", 0, "AV"), ("z1", 1, "AV"), ("out", 0, "V"), ("out", 1, "V")]


def number_jobs():
    table, n, emptied = {}, 0, {"A": 0, "V": 0}
    for name, half, engines in ORDER:
        for k in [k for k, job in enumerate(JOBS[name]) if job[0] == half]:
            engine = engines[k % len(engines)]
            emptied[engine] += 1
            table[name, k] = (n, emptied["A"], emptied["V"], engine)
            n += 1
    return table


NUMBERS = number_jobs()
BY_NUMBER = {v[0]: v for v in NUMBERS.values()}


def jobs_of(name, half, engine="AV"):
    return [(k, job[1:]) for k, job in enumerate(JOBS[name]) if job[0] == half and NUMBERS[name, k][3] in engine]


def last_of(name, half):
    return NUMBERS[name, jobs_of(name, half)[-1][0]]


def last_within(name, within):
    return NUMBERS[name, max(k for k, job in enumerate(JOBS[name]) if job[1].stop <= within.stop)]


PIECES = [HALVES[0], range(13, 19), range(19, 23), range(23, NT)]
NORMS = [HALVES, HALVES, [range(0, 8), range(8, 13), range(13, 21), range(21, NT)],
         [HALVES[0], range(13, 21), range(21, NT)]]


SHORT = 4


def node_cuts(ts):
    return (0, 112, NP) if len(ts) > SHORT else (0, NP)


def node_dmas(pieces):
    return sum(len(node_cuts(ts)) - 1 for ts in pieces)


def norm_events(n, piece):
    return sum(len(pieces) for pieces in NORMS[:n]) + piece + 1


def build(nc, x, srcg, dstT, dstrow, eaT, wqkv, wo, ff1w, ff1b, ff2w, weT, w1T, w2T, cols, rows,
          q_table, kv_table, h_table, rel_table, out):
    with ExitStack() as ctx:
        def sb(name, shape, dt=F32):
            return ctx.enter_context(nc.sbuf_tensor(name, shape, dt))

        def psum(name, shape):
            return ctx.enter_context(nc.psum_tensor(name, shape, F32))

        def sem(name):
            return ctx.enter_context(nc.semaphore(name))

        iota_w = sb("iota_w", [P, P])
        iota_p = sb("iota_p", [P, 1])
        ident = sb("ident", [P, P])
        eps_col = sb("eps_col", [P, 1])
        eps2_col = sb("eps2_col", [P, 1])
        zeros = sb("zeros", [P, D])
        wqkv_sb = sb("wqkv_sb", [D, 3 * D])
        wo_sb = sb("wo_sb", [D, D])
        ff1w_sb = sb("ff1w_sb", [D, FF])
        ff2w_sb = sb("ff2w_sb", [P, 2, D])
        weT_sb = sb("weT_sb", [EC + 1, D])
        w1T_sb = sb("w1T_sb", [D, D])
        w2T_sb = sb("w2T_sb", [D, D])
        cols_sb = sb("cols_sb", [D, 5])
        ff1b_sb = sb("ff1b_sb", [P, 2])
        rows_sb = sb("rows_sb", [P, 2, D])
        dstT_i = sb("dstT_i", [P, TILES], I32)
        base_i = sb("base_i", [P, TILES], I32)
        rel = sb("rel", [P, TILES])
        dst_rows = sb("dst_rows", [GROUPS, G, P], I32)
        rel_rows = sb("rel_rows", [GROUPS, G, P], BF16)
        minus_p = sb("minus_p", [P, 1])
        x_sb = sb("x_sb", [NP, NT, D])
        h_sb = sb("h_sb", [NP, NT, D])
        cen = sb("cen", [NP, NT, D])
        q_sb = sb("q_sb", [NP, NT, D])
        sq = q_sb
        rec_wide = cen
        kv_sb = sb("kv_sb", [NP, NT, 2 * D])
        x1_sb = sb("x1_sb", [NP, NT, D])
        stat = sb("stat", [NP, 7, NT])
        xnT = sb("xnT", [D, N])
        acc = sb("acc", [P, ACC_COLS])
        mT = sb("mT", [D, N])
        set_scratch = sb("set_scratch", [P, 1])
        rec = sb("rec", [NP, NT, H])
        ffT = sb("ffT", [P, 2, N])
        idx = [sb(f"idx{b}", [P, G], I32) for b in range(RING)]
        away = [sb(f"away{b}", [P, G * P], BF16) for b in range(2)]
        kv = [sb(f"kv{b}", [P, G, 2 * D]) for b in range(RING)]
        qwin = [sb(f"qwin{b}", [P, G, D]) for b in range(RING)]
        drow = [sb(f"drow{b}", [P, G * P], BF16) for b in range(RING)]
        ea = [sb(f"ea{b}", [EC + 1, G, P]) for b in range(RING)]
        spread = [sb(f"spread{b}", [P, G, P]) for b in range(2)]
        collect = [sb(f"collect{b}", [P, G, P]) for b in range(2)]
        prod = [sb(f"prod{b}", [P, G, D]) for b in range(2)]
        alpha = [sb(f"alpha{b}", [P, G * H]) for b in range(2)]
        vals = [sb(f"vals{b}", [P, G, VD]) for b in range(2)]

        ps_edge = [psum(f"ps_edge{b}", [P, 512]) for b in range(2)]
        ps_sum = [psum(f"ps_sum{b}", [P, G * P]) for b in range(2)]
        ps_node = [psum(f"ps_node{b}", [P, 512]) for b in range(2)]
        ps_spare = [psum(f"ps_spare{b}", [P, 512]) for b in range(2)]
        banks = [t[:, :] for t in ps_node + ps_edge + ps_sum + ps_spare]
        positions = ps_node[0][:, 0:P]
        weights = ps_node[1][:, 0:G * H]

        x_landed = [sem(f"x_landed{half}") for half in range(2)]
        weights_landed = sem("weights_landed")
        dst_landed = sem("dst_landed")
        dst_rows_landed = sem("dst_rows_landed")
        rel_stored = sem("rel_stored")
        rel_made = sem("rel_made")
        kv_stored = sem("kv_stored")
        q_stored = sem("q_stored")
        h_stored = sem("h_stored")
        out_stored = sem("out_stored")
        idx_landed = [sem(f"idx_landed{b}") for b in range(RING)]
        kv_landed = [sem(f"kv_landed{b}") for b in range(RING)]
        qwin_landed = [sem(f"qwin_landed{b}") for b in range(RING)]
        drow_landed = [sem(f"drow_landed{b}") for b in range(RING)]
        ea_landed = [sem(f"ea_landed{b}") for b in range(RING)]
        hg_landed = [sem(f"hg_landed{b}") for b in range(RING)]
        loads_begun = sem("loads_begun")
        gathers_begun = sem("gathers_begun")
        iotas_made = sem("iotas_made")
        consts_made = sem("consts_made")
        windows_made = sem("windows_made")
        acc_cleared = sem("acc_cleared")
        dve_chain = sem("dve_chain")
        variance_ready = sem("variance_ready")
        deviation_ready = sem("deviation_ready")
        normed = sem("normed")
        bank_filled = sem("bank_filled")
        emptied_act = sem("emptied_act")
        emptied_dve = sem("emptied_dve")
        centred = sem("centred")
        b2_added = sem("b2_added")
        rec_widened = sem("rec_widened")
        squared = sem("squared")
        unscaled_made = sem("unscaled_made")
        scales_made = sem("scales_made")
        h_scaled = sem("h_scaled")
        x_biased = sem("x_biased")
        residual_made = sem("residual_made")
        away_made = sem("away_made")
        spread_made = sem("spread_made")
        spread_used = sem("spread_used")
        collect_made = sem("collect_made")
        prod_made = sem("prod_made")
        alpha_made = sem("alpha_made")
        exp_made = sem("exp_made")
        weights_made = sem("weights_made")
        vals_made = sem("vals_made")
        summed = sem("summed")
        added = sem("added")
        emb_made = sem("emb_made")
        collect1_made = sem("collect1_made")
        message_made = sem("message_made")
        relu_made = sem("relu_made")
        summed1 = sem("summed1")
        added1 = sem("added1")

        def rounds(engine, body):
            body(0, True, False)
            with engine.Fori(1, ROUNDS - 1) as r:
                body(r, False, False)
            body(ROUNDS - 1, False, True)

        def by_nodes(engine, dst_rows, src_rows, signal, ts):
            cuts = node_cuts(ts)
            for a, b in zip(cuts, cuts[1:]):
                engine.dma_start(dst_rows[a:b], src_rows[a:b]).then_inc(signal, 16)

        def dram_nodes(table, ts):
            return table[0:N, :].rearrange("(p t) d -> p t d", t=NT)[:, ts.start:ts.stop, :]

        def sbuf_nodes(tensor, ts):
            return tensor[:, ts.start:ts.stop, :]

        def by_columns_of(tensor, ts):
            return tensor[0:D, 0:N].rearrange("d (p t) -> d t p", t=NT)[:, ts.start:ts.stop, :]

        def as_columns(bank, ts):
            return bank[0:D, 0:len(ts) * NP].rearrange("d (t p) -> d t p", p=NP)

        def halves_done(half):
            return half + 1

        block = ctx.enter_context(nc.Block())

        @block.sync
        def _(sp):
            for half, ts in enumerate(HALVES):
                by_nodes(sp, sbuf_nodes(x_sb, ts), dram_nodes(x, ts), x_landed[half], ts)
            sp.dma_start(dst_rows[:, :, :], dstrow[:, :, :]).then_inc(dst_rows_landed, 16)
            sp.dma_start(dstT_i[:, :], dstT[:, :]).then_inc(dst_landed, 16)
            sp.dma_start(base_i[:, :], dstT[0:1, :].partition_broadcast(P)).then_inc(dst_landed, 16)
            for b in range(RING):
                sp.dma_start(idx[b][:, :], srcg[b]).then_inc(idx_landed[b], 16)
                sp.dma_start(ea[b][:, :, :], eaT[b]).then_inc(ea_landed[b], 16)

            sp.wait_ge(rel_made, 1)
            sp.dma_start(rel_table[:, :], rel_rows[:, :, :].rearrange("g j e -> g (j e)")).then_inc(rel_stored, 16)

            def load_rows(slots):
                for b in slots:
                    sp.dma_start(drow[b][:, :], rel_table[b:b + 1, :].partition_broadcast(P)
                                 ).then_inc(drow_landed[b], 16)

            for piece, ts in enumerate(PIECES):
                last_job = max(k for k, (_, us) in enumerate(QBLOCKS) if us.start < ts.stop)
                _, n_act, n_dve, _ = NUMBERS["qkv", last_job]
                sp.wait_ge(emptied_act, n_act)
                sp.wait_ge(emptied_dve, n_dve)
                by_nodes(sp, dram_nodes(kv_table, ts), sbuf_nodes(kv_sb, ts), kv_stored, ts)
                if piece == 0:
                    sp.wait_ge(rel_stored, 16)
                    load_rows(range(RING // 2))
            by_nodes(sp, dram_nodes(q_table, range(NT)), sbuf_nodes(q_sb, range(NT)), q_stored, range(NT))
            sp.wait_ge(consts_made, 1)
            sp.dma_start(q_table[N:N + P, :], zeros[:, :]).then_inc(q_stored, 16)
            load_rows(range(RING // 2, RING))

            def load_windows(group, b, slot_free):
                _, bases = nc.values_load_multi_w_load_instructions(
                    base_i[0:1, bass.ds(group * G, G)], engines=[ET.SP], min_val=0, max_val=N - 1,
                    skip_runtime_bounds_check_because="dst is a node's number, the first of a tile never padding")
                slot_free()
                for j in range(G):
                    sp.dma_start(qwin[b][:, j, :], q_table[bass.ds(bases[j], P), :]).then_inc(qwin_landed[b], 16)

            sp.wait_ge(q_stored, 16 * 3)
            sp.wait_ge(dst_landed, 32)
            for b in range(RING):
                load_windows(b, b, lambda: None)

            def next_inputs(r, first, last):
                if last:
                    return
                for b in range(RING):
                    group = r * RING + b
                    sp.wait_ge(kv_landed[b], 16 * G * (r + 1))
                    sp.dma_start(idx[b][:, :], srcg[bass.ds(group + RING, 1)].rearrange("a p j -> (a p) j")
                                 ).then_inc(idx_landed[b], 16)
                    sp.wait_ge(spread_made, group + 1)
                    sp.sem_inc(loads_begun, 1)
                    sp.dma_start(drow[b][:, :], rel_table[bass.ds(group + RING, 1), :].partition_broadcast(P)
                                 ).then_inc(drow_landed[b], 16)
                    load_windows(group + RING, b, lambda: sp.wait_ge(spread_used, group + 1))

            rounds(sp, next_inputs)

            for b in range(RING):
                sp.wait_ge(kv_landed[b], 16 * G * ROUNDS)
                sp.dma_start(idx[b][:, :], srcg[b]).then_inc(idx_landed[b], 16)

            for piece, ts in enumerate(NORMS[3]):
                sp.wait_ge(normed, norm_events(3, piece) - len(NORMS[0]))
                by_nodes(sp, dram_nodes(h_table, ts), sbuf_nodes(h_sb, ts), h_stored, ts)

            def next_inputs1(r, first, last):
                if last:
                    return
                for b in range(RING):
                    group = r * RING + b
                    sp.wait_ge(hg_landed[b], 16 * G * (r + 1))
                    sp.dma_start(idx[b][:, :], srcg[bass.ds(group + RING, 1)].rearrange("a p j -> (a p) j")
                                 ).then_inc(idx_landed[b], 16)
                    sp.wait_ge(emb_made, group + 1)
                    sp.dma_start(ea[b][:, :, :], eaT[bass.ds(group + RING, 1)].rearrange("a c j e -> (a c) j e")
                                 ).then_inc(ea_landed[b], 16)

            rounds(sp, next_inputs1)

            for k, (_, ts) in enumerate(TBLOCKS):
                sp.wait_ge(emptied_dve, NUMBERS["out", k][2])
                by_nodes(sp, dram_nodes(out, ts), sbuf_nodes(h_sb, ts), out_stored, ts)
            sp.wait_ge(out_stored, 16 * node_dmas([ts for _, ts in TBLOCKS]))

        @block.gpsimd
        def _(pool):
            nc.gpsimd.iota(iota_w[:, :], [[1, P]], base=0, channel_multiplier=0,
                           allow_small_or_imprecise_dtypes=True).then_inc(iotas_made, 1)
            nc.gpsimd.iota(iota_p[:, :], [[0, 1]], base=0, channel_multiplier=1,
                           allow_small_or_imprecise_dtypes=True).then_inc(iotas_made, 1)

            def load(dst, src):
                pool.dma_start(dst, src).then_inc(weights_landed, 16)

            load(cols_sb[:, :], cols[:, :])
            load(wqkv_sb[:, :], wqkv[:, :])
            load(wo_sb[:, :], wo[:, :])
            load(ff1w_sb[:, :], ff1w[:, :])
            load(ff1b_sb[:, :], ff1b[:, :])
            load(ff2w_sb[:, :, :], ff2w[:, :].rearrange("(c p) n -> p c n", p=P))
            load(rows_sb[:, :, :], rows[:, :, :].partition_broadcast(P))
            load(weT_sb[:, :], weT[:, :])
            load(w1T_sb[:, :], w1T[:, :])
            load(w2T_sb[:, :], w2T[:, :])

            pool.wait_ge(iotas_made, 2)
            nc.gpsimd.memset(acc[0:D, :], 0.0).then_inc(acc_cleared, 1)
            pool.wait_ge(acc_cleared, 1)
            nc.gpsimd.memset(acc[D:VD, :], DEN_EPS).then_inc(acc_cleared, 1)
            pool.wait_ge(acc_cleared, 2)
            pool.wait_ge(weights_landed, 16 * WEIGHT_DMAS)
            for half, ts in enumerate(HALVES):
                pool.wait_ge(centred, norm_events(0, half))
                nc.gpsimd.tensor_tensor(sbuf_nodes(x_sb, ts), sbuf_nodes(x_sb, ts),
                                        rows_sb[0:NP, 0:1, :].to_broadcast([NP, len(ts), D]),
                                        ALU.add).then_inc(x_biased, 1)

            def gather(r, b, table, width, landed):
                for j in range(G):
                    pool.indirect_dma_start(
                        out=kv[b][:, j, 0:width], out_offset=None, in_=table,
                        in_offset=bass.IndirectOffsetOnAxis(ap=idx[b][:, j:j + 1], axis=0)).then_inc(landed[b], 16)

            def gather_kv(r, first, last):
                for b in range(RING):
                    pool.wait_ge(idx_landed[b], 16 * (r + 1))
                    if not first:
                        pool.wait_ge(vals_made, (r - 1) * RING + b + 1)
                    pool.sem_inc(gathers_begun, 1)
                    gather(r, b, kv_table[:, :], 2 * D, kv_landed)

            pool.wait_ge(scales_made, 1)
            nc.gpsimd.tensor_tensor(h_sb[:, :, :], h_sb[:, :, :],
                                    stat[:, 6, :].unsqueeze(2).to_broadcast([NP, NT, D]),
                                    ALU.mult).then_inc(h_scaled, 1)

            pool.wait_ge(kv_stored, 16 * node_dmas(PIECES))
            rounds(pool, gather_kv)

            def gather_h(r, first, last):
                for b in range(RING):
                    pool.wait_ge(idx_landed[b], 16 * (ROUNDS + r + 1))
                    if not first:
                        pool.wait_ge(message_made, (r - 1) * RING + b + 1)
                    pool.sem_inc(gathers_begun, 1)
                    gather(r, b, h_table[:, :], D, hg_landed)

            pool.wait_ge(x_biased, 2)
            for half, ts in enumerate(HALVES):
                pool.wait_ge(centred, norm_events(2, 2 * half + 1))
                nc.gpsimd.tensor_tensor(sbuf_nodes(x1_sb, ts), sbuf_nodes(x1_sb, ts), sbuf_nodes(x_sb, ts),
                                        ALU.add).then_inc(residual_made, 1)

            pool.wait_ge(h_stored, 16 * node_dmas(NORMS[3]))
            rounds(pool, gather_h)

        @block.tensor
        def _(pe):
            def columns_made(name, ts):
                emptied(NUMBERS[name, max(k for k, job in enumerate(JOBS[name]) if job[1].start < ts.stop)])

            def keep_warm(products, bank=ps_spare[1][:, :]):
                for _ in range(products):
                    nc.tensor.matmul(bank, ident[:, :],
                                     iota_w[:, :].unsqueeze(1).to_broadcast([P, 4, P]), start=True, stop=True)

            def emptied(job):
                _, n_act, n_dve, _ = job
                if n_act:
                    pe.wait_ge(emptied_act, n_act)
                if n_dve:
                    pe.wait_ge(emptied_dve, n_dve)

            def bank_of(name, k):
                n = NUMBERS[name, k][0]
                if n >= len(banks):
                    emptied(BY_NUMBER[n - len(banks)])
                return banks[n % len(banks)]

            def transposes(name, half, source, norm):
                for k, (ts,) in jobs_of(name, half):
                    pe.wait_ge(normed, -len(NORMS[0]) + norm_events(norm, max(i for i, piece in enumerate(NORMS[norm])
                                                             if piece.start < ts.stop)))
                    bank = bank_of(name, k)
                    for i, t in enumerate(ts):
                        last = nc.tensor.transpose(bank[0:D, i * NP:(i + 1) * NP], source[:, t, :],
                                                   ident[0:NP, 0:NP])
                    last.then_inc(bank_filled, 1)

            def by_columns(name, half, source, made_by, weights_sb, width):
                for k, (ts,) in jobs_of(name, half):
                    bank = bank_of(name, k)
                    columns_made(made_by, ts)
                    for i, t in enumerate(ts):
                        last = nc.tensor.matmul(bank[0:NP, i * width:(i + 1) * width],
                                                source[:, t * NP:(t + 1) * NP], weights_sb[:, :],
                                                start=True, stop=True)
                    last.then_inc(bank_filled, 1)

            pe.wait_ge(consts_made, 1)
            pe.wait_ge(squared, norm_events(1, 0))
            keep_warm(WARM_UPS["xnT"])
            pe.wait_ge(weights_landed, 16 * WEIGHT_DMAS)
            for half in range(2):
                transposes("xnT", half, cen, 1)
                by_columns("qkv", half, xnT, "xnT", wqkv_sb, 3 * D)

            def expand(r, b, first):
                group = r * RING + b
                pe.wait_ge(spread_made, group + 1)
                pe.wait_ge(qwin_landed[b], 16 * G * (r + 1))
                if not (first and b < 2):
                    pe.wait_ge(prod_made, group - 1)
                for j in range(G):
                    last = nc.tensor.matmul(ps_edge[b % 2][:, j * D:(j + 1) * D], spread[b % 2][:, j, :],
                                            qwin[b][:, j, :], start=True, stop=True)
                last.then_inc(spread_used, 1)

            def edges0(r, first, last_round):
                if first:
                    expand(0, 0, True)
                for b in range(RING):
                    group = r * RING + b
                    if b + 1 < RING:
                        expand(r, b + 1, first)
                    elif not last_round:
                        expand(r + 1, 0, False)
                    if last_round and b == RING - 1:
                        keep_warm(WARM_UPS["last sums"])
                    pe.wait_ge(vals_made, group + 1)
                    pe.wait_ge(weights_made, group + 1)
                    pe.wait_ge(collect_made, group + 1)
                    if not (first and b < 2):
                        pe.wait_ge(added, G * (group - 1))
                    for j in range(G):
                        last = nc.tensor.matmul(ps_sum[b % 2][0:VD, j * P:(j + 1) * P], vals[b % 2][:, j, :],
                                                collect[b % 2][:, j, :], start=True, stop=True)
                    last.then_inc(summed, 1)

            emptied(last_of("qkv", 1))
            rounds(pe, edges0)

            keep_warm(WARM_UPS["den"])
            pe.wait_ge(added, G * GROUPS)
            for half in range(2):
                for k, (ts,) in jobs_of("den", half):
                    bank = bank_of("den", k)
                    for i, t in enumerate(ts):
                        last = nc.tensor.transpose(bank[0:NP, i * H:(i + 1) * H], acc[D:VD, t:N:NT],
                                                   ident[D:VD, D:VD])
                    last.then_inc(bank_filled, 1)
            keep_warm(WARM_UPS["recT"], bank_of("recT", 0))
            for half in range(2):
                pe.wait_ge(rec_widened, halves_done(half))
                for k, (ts,) in jobs_of("recT", half):
                    bank = bank_of("recT", k)
                    for i, t in enumerate(ts):
                        last = nc.tensor.transpose(bank[0:D, i * NP:(i + 1) * NP],
                                                   rec_wide[:, t, :],
                                                   ident[0:NP, 0:NP])
                    last.then_inc(bank_filled, 1)
            for half in range(2):
                by_columns("attn", half, mT, "recT", wo_sb, D)

            def ff1(half):
                for k, (ts, c) in jobs_of("ff1", half):
                    bank = bank_of("ff1", k)
                    emptied(NUMBERS["xn2T", k // 2])
                    nc.tensor.matmul(bank[:, 0:len(ts) * NP], ff1w_sb[:, c * P:(c + 1) * P],
                                     xnT[:, ts.start * NP:ts.stop * NP], start=True, stop=True
                                     ).then_inc(bank_filled, 1)

            def ff2(half):
                for k, (ts,) in jobs_of("ff2", half):
                    bank = bank_of("ff2", k)
                    columns_made("ff1", ts)
                    for i, t in enumerate(ts):
                        for c in range(2):
                            last = nc.tensor.matmul(bank[0:NP, i * D:(i + 1) * D], ffT[:, c, t * NP:(t + 1) * NP],
                                                    ff2w_sb[:, c, :], start=(c == 0), stop=(c == 1))
                    last.then_inc(bank_filled, 1)

            keep_warm(WARM_UPS["xn2T"], bank_of("xn2T", jobs_of("xn2T", 0)[0][0]))
            transposes("xn2T", 0, cen, 2)
            ff1(0)
            transposes("xn2T", 1, cen, 2)
            ff2(0)
            ff1(1)
            ff2(1)
            for half in range(2):
                transposes("h1T", half, h_sb, 3)

            def embed(r, b, first):
                group = r * RING + b
                pe.wait_ge(ea_landed[b], 16 * (r + 1))
                if not (first and b < 2):
                    pe.wait_ge(message_made, group - 1)
                for j in range(G):
                    last = nc.tensor.matmul(ps_edge[b % 2][:, j * D:(j + 1) * D], ea[b][:, j, :],
                                            weT_sb[:, :], start=True, stop=True)
                last.then_inc(emb_made, 1)

            def edges1(r, first, last_round):
                if first:
                    embed(0, 0, True)
                for b in range(RING):
                    group = r * RING + b
                    if b + 1 < RING:
                        embed(r, b + 1, first)
                    elif not last_round:
                        embed(r + 1, 0, False)
                    if last_round and b == RING - 1:
                        keep_warm(WARM_UPS["last sums 1"])
                    pe.wait_ge(relu_made, group + 1)
                    pe.wait_ge(collect1_made, group + 1)
                    if not (first and b < 2):
                        pe.wait_ge(added1, G * (group - 1))
                    for j in range(G):
                        last = nc.tensor.matmul(ps_sum[b % 2][0:D, j * P:(j + 1) * P], vals[b % 2][:, j, 0:D],
                                                collect[b % 2][:, j, :], start=True, stop=True)
                    last.then_inc(summed1, 1)

            emptied(last_of("h1T", 1))
            rounds(pe, edges1)

            keep_warm(WARM_UPS["z1"])
            pe.wait_ge(added1, G * GROUPS)
            for half in range(2):
                for k, (ts,) in jobs_of("z1", half):
                    bank = bank_of("z1", k)
                    nc.tensor.matmul(bank[0:D, 0:len(ts) * NP], w1T_sb[:, :],
                                     by_columns_of(acc, ts), start=True, stop=True).then_inc(bank_filled, 1)
            for half in range(2):
                by_columns("out", half, mT, "z1", w2T_sb, D)

        @block.scalar
        def _(act):
            def squares(n, piece):
                ts = NORMS[n][piece]
                act.wait_ge(centred, norm_events(n, piece))
                nc.scalar.activation(sbuf_nodes(sq, ts), sbuf_nodes(cen, ts), ACT.Square).then_inc(squared, 1)

            def deviations(n, piece):
                ts = NORMS[n][piece]
                act.wait_ge(variance_ready, norm_events(n, piece))
                source, result, guard = {0: (1, 5, eps_col), 1: (2, 3, eps2_col)}.get(n, (2, 3, eps_col))
                nc.scalar.activation(stat[:, result, ts.start:ts.stop], stat[:, source, ts.start:ts.stop], ACT.Sqrt,
                                     bias=guard[0:NP, :], scale=1.0 / D).then_inc(deviation_ready, 1)

            def fetch_sqrt():
                nc.scalar.activation(set_scratch[:, :], eps_col[:, :], ACT.Sqrt)

            def filled(name, k):
                n = NUMBERS[name, k][0]
                act.wait_ge(bank_filled, n + 1)
                return banks[n % len(banks)]

            def scaled_transpose(name, k, ts, g, b):
                bank = filled(name, k)
                nc.scalar.activation(xnT[:, ts.start * NP:ts.stop * NP], bank[0:D, 0:len(ts) * NP],
                                     ACT.Identity, bias=cols_sb[:, b:b + 1], scale=cols_sb[:, g:g + 1]
                                     ).then_inc(emptied_act, 1)

            act.wait_ge(consts_made, 1)
            fetch_sqrt()
            for half, ts in enumerate(HALVES):
                act.wait_ge(centred, norm_events(0, half))
                nc.scalar.activation(sbuf_nodes(h_sb, ts), sbuf_nodes(cen, ts), ACT.Relu).then_inc(unscaled_made, 1)
                squares(0, half)
            act.wait_ge(variance_ready, norm_events(0, 0))
            squares(1, 0)
            deviations(1, 0)
            squares(1, 1)
            deviations(1, 1)
            deviations(0, 0)
            deviations(0, 1)
            act.wait_ge(weights_landed, 16 * WEIGHT_DMAS)
            for half in range(2):
                for k, (ts,) in jobs_of("xnT", half, "A"):
                    scaled_transpose("xnT", k, ts, 0, 1)
                for k, (ts,) in jobs_of("qkv", half, "A"):
                    bank = filled("qkv", k)
                    view = bank[0:NP, 0:len(ts) * 3 * D].rearrange("p (t c) -> p t c", c=3 * D)
                    nc.scalar.activation(sbuf_nodes(q_sb, ts), view[:, :, 0:D], ACT.Copy, scale=HD ** -0.5)
                    nc.scalar.activation(sbuf_nodes(kv_sb, ts), view[:, :, D:3 * D], ACT.Copy
                                         ).then_inc(emptied_act, 1)

            def make_spread(r, b, first):
                group = r * RING + b
                act.wait_ge(drow_landed[b], 16 * (r + 1))
                nc.scalar.activation(away[b % 2][:, :], drow[b][:, :], ACT.Abs,
                                     bias=minus_p[:, :]).then_inc(away_made, 1)
                if not (first and b < 2):
                    act.wait_ge(spread_used, group - 1)
                act.wait_ge(away_made, group + 1)
                nc.scalar.activation(spread[b % 2][:, :, :].rearrange("p j e -> p (j e)"), away[b % 2][:, :], ACT.Relu,
                                     bias=1.0, scale=-1.0).then_inc(spread_made, 1)

            def exps(r, first, last):
                if first:
                    make_spread(0, 0, True)
                for b in range(RING):
                    group = r * RING + b
                    if b + 1 < RING:
                        make_spread(r, b + 1, first)
                    elif not last:
                        make_spread(r + 1, 0, False)
                    act.wait_ge(alpha_made, group + 1)
                    if not (first and b == 0):
                        act.wait_ge(vals_made, group)
                    nc.scalar.activation(weights, alpha[b % 2][:, :], ACT.Exp).then_inc(exp_made, 1)
                    if not (first and b < 2):
                        act.wait_ge(summed, group - 1)
                    nc.scalar.activation(vals[b % 2][:, :, D:VD],
                                         alpha[b % 2][:, :].rearrange("p (j h) -> p j h", h=H),
                                         ACT.Exp).then_inc(weights_made, 1)

            act.wait_ge(emptied_act, last_of("qkv", 1)[1])
            act.wait_ge(emptied_dve, last_of("qkv", 1)[2])
            rounds(act, exps)

            def relu_of(k, ts, c):
                bank = filled("ff1", k)
                nc.scalar.activation(ffT[:, c, ts.start * NP:ts.stop * NP], bank[:, 0:len(ts) * NP], ACT.Relu,
                                     bias=ff1b_sb[:, c:c + 1]).then_inc(emptied_act, 1)

            fetch_sqrt()
            for half, ts in enumerate(HALVES):
                act.wait_ge(emptied_dve, last_of("den", half)[2])
                nc.scalar.activation(sbuf_nodes(rec_wide, ts).rearrange("p t (h c) -> p t h c", c=HD),
                                     sbuf_nodes(rec, ts).unsqueeze(3).to_broadcast([NP, len(ts), H, HD]),
                                     ACT.Copy).then_inc(rec_widened, 1)
            squares(2, 0)
            squares(2, 1)
            deviations(2, 0)
            deviations(2, 1)
            for step, (k, (ts,)) in enumerate(jobs_of("xn2T", 0, "A")):
                if step == 2:
                    squares(2, 2)
                if step == 3:
                    squares(2, 3)
                scaled_transpose("xn2T", k, ts, 2, 3)
            deviations(2, 2)
            deviations(2, 3)
            for k, (ts, c) in jobs_of("ff1", 0, "A"):
                relu_of(k, ts, c)
            for k, (ts,) in jobs_of("xn2T", 1, "A"):
                scaled_transpose("xn2T", k, ts, 2, 3)
            for step, (k, (ts, c)) in enumerate(jobs_of("ff1", 1, "A")):
                if step == 3:
                    squares(3, 0)
                if step == 5:
                    deviations(3, 0)
                relu_of(k, ts, c)
            squares(3, 1)
            deviations(3, 1)
            squares(3, 2)
            deviations(3, 2)
            for half in range(2):
                for k, (ts,) in jobs_of("h1T", half, "A"):
                    bank = filled("h1T", k)
                    nc.scalar.activation(by_columns_of(acc, ts), as_columns(bank, ts), ACT.Copy
                                         ).then_inc(emptied_act, 1)

            def relus(r, first, last):
                for b in range(RING):
                    group = r * RING + b
                    act.wait_ge(message_made, group + 1)
                    if not (first and b < 2):
                        act.wait_ge(summed1, group - 1)
                    nc.scalar.activation(vals[b % 2][:, :, 0:D], prod[b % 2][:, :, :],
                                         ACT.Relu).then_inc(relu_made, 1)

            rounds(act, relus)

            for half in range(2):
                for k, (ts,) in jobs_of("z1", half, "A"):
                    bank = filled("z1", k)
                    nc.scalar.activation(mT[:, ts.start * NP:ts.stop * NP], bank[0:D, 0:len(ts) * NP], ACT.Relu,
                                         bias=cols_sb[:, 4:5]).then_inc(emptied_act, 1)

        @block.vector
        def _(dve):
            done = [0]

            def link(ins):
                done[0] += 1
                ins.then_inc(dve_chain, 1)
                dve.wait_ge(dve_chain, done[0])

            nc.vector.memset(eps_col[:, :], EPS)
            nc.vector.memset(eps2_col[:, :], EPS * EPS)
            nc.vector.memset(zeros[:, :], 0.0)
            dve.wait_ge(iotas_made, 2)
            nc.vector.tensor_scalar(minus_p[:, :], iota_p[:, :], -1.0, None, ALU.mult)
            nc.vector.tensor_tensor(ident[:, :], iota_w[:, :], iota_p[:, 0:1].to_broadcast([P, P]),
                                    ALU.is_equal).then_inc(consts_made, 1)

            def over_features(column, ts):
                return stat[:, column, ts.start:ts.stop].unsqueeze(2).to_broadcast([NP, len(ts), D])

            def norm_centre(n, piece, source):
                ts = NORMS[n][piece]
                link(nc.vector.tensor_reduce(stat[:, 0, ts.start:ts.stop], sbuf_nodes(source, ts), AX.X, ALU.add))
                nc.vector.scalar_tensor_tensor(sbuf_nodes(cen, ts), over_features(0, ts), -1.0 / D,
                                               sbuf_nodes(source, ts), ALU.mult, ALU.add).then_inc(centred, 1)

            def norm_variance(n, piece):
                ts = NORMS[n][piece]
                dve.wait_ge(squared, norm_events(n, piece))
                sums = nc.vector.tensor_reduce(stat[:, 1 if n == 0 else 2, ts.start:ts.stop], sbuf_nodes(sq, ts),
                                               AX.X, ALU.add)
                if n == 1:
                    link(sums)
                    sums = nc.vector.scalar_tensor_tensor(stat[:, 2, ts.start:ts.stop], stat[:, 1, ts.start:ts.stop],
                                                          EPS, stat[:, 2, ts.start:ts.stop], ALU.mult, ALU.add)
                sums.then_inc(variance_ready, 1)

            def norm_scale(n, piece, result, op0, scalar):
                ts = NORMS[n][piece]
                dve.wait_ge(deviation_ready, norm_events(n, piece) - (len(NORMS[0]) if n == 1 else 0))
                link(nc.vector.reciprocal(stat[:, 4, ts.start:ts.stop], stat[:, 3, ts.start:ts.stop]))
                nc.vector.scalar_tensor_tensor(sbuf_nodes(result, ts), sbuf_nodes(cen, ts), scalar,
                                               over_features(4, ts), op0, ALU.mult).then_inc(normed, 1)

            def filled(name, k):
                n = NUMBERS[name, k][0]
                dve.wait_ge(bank_filled, n + 1)
                return banks[n % len(banks)]

            dve.wait_ge(x_landed[0], 32)
            norm_centre(0, 0, x_sb)
            dve.wait_ge(x_landed[1], 32)
            norm_centre(0, 1, x_sb)
            norm_variance(0, 0)
            dve.wait_ge(unscaled_made, 1)
            norm_centre(1, 0, h_sb)
            norm_variance(0, 1)
            norm_variance(1, 0)
            dve.wait_ge(unscaled_made, 2)
            norm_centre(1, 1, h_sb)
            norm_scale(1, 0, cen, ALU.mult, 1.0)
            norm_variance(1, 1)
            norm_scale(1, 1, cen, ALU.mult, 1.0)
            dve.wait_ge(deviation_ready, norm_events(1, 1))
            nc.vector.reciprocal(stat[:, 6, :], stat[:, 5, :]).then_inc(scales_made, 1)

            dve.wait_ge(weights_landed, 16 * WEIGHT_DMAS)

            def scaled_transposes(name, half, g, b):
                for k, (ts,) in jobs_of(name, half, "V"):
                    bank = filled(name, k)
                    nc.vector.tensor_scalar(xnT[:, ts.start * NP:ts.stop * NP], bank[0:D, 0:len(ts) * NP],
                                            cols_sb[:, g:g + 1], cols_sb[:, b:b + 1], ALU.mult, ALU.add
                                            ).then_inc(emptied_dve, 1)

            for half in range(2):
                scaled_transposes("xnT", half, 0, 1)
                if half == 0:
                    dve.wait_ge(dst_rows_landed, 16)
                    nc.vector.tensor_tensor(rel_rows[:, :, :], dst_rows[:, :, :],
                                            dst_rows[:, :, 0:1].to_broadcast([GROUPS, G, P]), ALU.subtract
                                            ).then_inc(rel_made, 1)
                for k, (ts,) in jobs_of("qkv", half, "V"):
                    bank = filled("qkv", k)
                    view = bank[0:NP, 0:len(ts) * 3 * D].rearrange("p (t c) -> p t c", c=3 * D)
                    nc.vector.tensor_scalar(sbuf_nodes(q_sb, ts), view[:, :, 0:D], HD ** -0.5, None, ALU.mult)
                    nc.vector.tensor_copy(sbuf_nodes(kv_sb, ts), view[:, :, D:3 * D]).then_inc(emptied_dve, 1)

            dve.wait_ge(dst_landed, 32)
            nc.vector.tensor_tensor(rel[:, :], dstT_i[:, :], base_i[:, :], ALU.subtract).then_inc(windows_made, 1)
            dve.wait_ge(emptied_act, last_of("qkv", 1)[1])
            dve.wait_ge(emptied_dve, last_of("qkv", 1)[2])
            dve.wait_ge(windows_made, 1)
            link(nc.vector.tensor_copy(positions, iota_w[:, :]))

            def make_collect(r, b, first, used, made):
                group = r * RING + b
                if not (first and b < 2):
                    dve.wait_ge(used, group - 1)
                nc.vector.tensor_tensor(collect[b % 2][:, :, :],
                                        positions.unsqueeze(1).to_broadcast([P, G, P]),
                                        rel[:, bass.ds(group * G, G)].unsqueeze(2).to_broadcast([P, G, P]),
                                        ALU.is_equal).then_inc(made, 1)

            def add_windows(group, b, rows, was_summed, was_added, none_before):
                _, bases = nc.values_load_multi_w_load_instructions(
                    base_i[0:1, bass.ds(group * G, G)], engines=[ET.DVE], min_val=0, max_val=N - 1,
                    skip_runtime_bounds_check_because="dst is a node's number, the first of a tile never padding")
                dve.wait_ge(was_summed, group + 1)
                for j in range(G):
                    if not (none_before and j == 0):
                        dve.wait_ge(was_added, group * G + j)
                    window = acc[0:rows, bass.ds(bases[j], P)]
                    nc.vector.tensor_tensor(window, window, ps_sum[b % 2][0:rows, j * P:(j + 1) * P],
                                            ALU.add).then_inc(was_added, 1)

            def edges0(r, first, last_round):
                for b in range(RING):
                    group = r * RING + b
                    make_collect(r, b, first, summed, collect_made)
                    dve.wait_ge(kv_landed[b], 16 * G * (r + 1))
                    dve.wait_ge(spread_used, group + 1)
                    nc.vector.tensor_tensor(prod[b % 2][:, :, :],
                                            ps_edge[b % 2][:, 0:G * D].rearrange("p (j c) -> p j c", c=D),
                                            kv[b][:, :, 0:D], ALU.mult).then_inc(prod_made, 1)
                    dve.wait_ge(prod_made, group + 1)
                    if not (first and b < 2):
                        dve.wait_ge(weights_made, group - 1)
                    nc.vector.tensor_reduce(alpha[b % 2][:, :],
                                            prod[b % 2][:, :, :].rearrange("p j (h c) -> p (j h) c", c=HD),
                                            AX.X, ALU.add).then_inc(alpha_made, 1)
                    dve.wait_ge(exp_made, group + 1)
                    if not (first and b < 2):
                        dve.wait_ge(summed, group - 1)
                    nc.vector.tensor_tensor(vals[b % 2][:, :, 0:D].rearrange("p j (h c) -> p j h c", c=HD),
                                            kv[b][:, :, D:2 * D].rearrange("p j (h c) -> p j h c", c=HD),
                                            weights.rearrange("p (j h) -> p j h", h=H).unsqueeze(3)
                                            .to_broadcast([P, G, H, HD]),
                                            ALU.mult).then_inc(vals_made, 1)
                    if not (first and b == 0):
                        add_windows(group - 1, (b - 1) % 2, VD, summed, added, first and b == 1)

            dve.wait_ge(acc_cleared, 2)
            rounds(dve, edges0)
            add_windows(GROUPS - 1, (RING - 1) % 2, VD, summed, added, False)

            for half in range(2):
                for k, (ts,) in jobs_of("den", half, "V"):
                    bank = filled("den", k)
                    nc.vector.reciprocal(sbuf_nodes(rec, ts),
                                         bank[0:NP, 0:len(ts) * H].rearrange("p (t h) -> p t h", h=H)
                                         ).then_inc(emptied_dve, 1)
            dve.wait_ge(added, G * GROUPS)
            for half in range(2):
                for k, (ts,) in jobs_of("recT", half, "V"):
                    bank = filled("recT", k)
                    nc.vector.tensor_tensor(mT[:, ts.start * NP:ts.stop * NP].rearrange("d (t p) -> d t p", p=NP),
                                            by_columns_of(acc, ts), as_columns(bank, ts),
                                            ALU.mult).then_inc(emptied_dve, 1)

            def add_banks(name, within, result, other):
                for k, (half, ts) in enumerate(JOBS[name]):
                    if not (ts.start >= within.start and ts.stop <= within.stop):
                        continue
                    bank = filled(name, k)
                    nc.vector.tensor_tensor(sbuf_nodes(result, ts),
                                            bank[0:NP, 0:len(ts) * D].rearrange("p (t d) -> p t d", d=D),
                                            sbuf_nodes(other, ts), ALU.add).then_inc(emptied_dve, 1)

            def relus_of(half):
                for k, (ts, c) in jobs_of("ff1", half, "V"):
                    bank = filled("ff1", k)
                    nc.vector.tensor_scalar(ffT[:, c, ts.start * NP:ts.stop * NP], bank[:, 0:len(ts) * NP],
                                            ff1b_sb[:, c:c + 1], 0.0, ALU.add, ALU.max).then_inc(emptied_dve, 1)

            dve.wait_ge(h_scaled, 1)
            def attention_added(piece):
                add_banks("attn", NORMS[2][piece], x1_sb, h_sb)

            for piece in range(2):
                attention_added(piece)
                dve.wait_ge(emptied_dve, last_within("attn", NORMS[2][piece])[2])
                norm_centre(2, piece, x1_sb)
            norm_variance(2, 0)
            norm_variance(2, 1)
            attention_added(2)
            norm_scale(2, 0, cen, ALU.mult, 1.0)
            norm_scale(2, 1, cen, ALU.mult, 1.0)
            attention_added(3)
            for piece in range(2, 4):
                dve.wait_ge(emptied_dve, last_within("attn", NORMS[2][piece])[2])
                norm_centre(2, piece, x1_sb)
            norm_variance(2, 2)
            norm_variance(2, 3)
            norm_scale(2, 2, cen, ALU.mult, 1.0)
            norm_scale(2, 3, cen, ALU.mult, 1.0)

            relus_of(0)
            scaled_transposes("xn2T", 1, 2, 3)
            relus_of(1)
            def result_centred(piece):
                dve.wait_ge(residual_made, halves_done(min(piece, 1)))
                add_banks("ff2", NORMS[3][piece], x_sb, x1_sb)
                dve.wait_ge(emptied_dve, last_within("ff2", NORMS[3][piece])[2])
                norm_centre(3, piece, x_sb)

            result_centred(0)
            norm_variance(3, 0)
            norm_scale(3, 0, h_sb, ALU.max, 0.0)
            result_centred(1)
            norm_variance(3, 1)
            norm_scale(3, 1, h_sb, ALU.max, 0.0)
            result_centred(2)
            norm_variance(3, 2)
            norm_scale(3, 2, h_sb, ALU.max, 0.0)
            for half in range(2):
                for k, (ts,) in jobs_of("h1T", half, "V"):
                    bank = filled("h1T", k)
                    nc.vector.tensor_copy(by_columns_of(acc, ts), as_columns(bank, ts)).then_inc(emptied_dve, 1)
            dve.wait_ge(centred, norm_events(3, 2))
            nc.vector.tensor_tensor(x_sb[:, :, :], x_sb[:, :, :], rows_sb[0:NP, 1:2, :].to_broadcast([NP, NT, D]),
                                    ALU.add).then_inc(b2_added, 1)

            dve.wait_ge(emptied_act, last_of("h1T", 1)[1])
            dve.wait_ge(emptied_dve, last_of("h1T", 1)[2])
            link(nc.vector.tensor_copy(positions, iota_w[:, :]))

            def edges1(r, first, last_round):
                for b in range(RING):
                    group = r * RING + b
                    make_collect(r, b, first, summed1, collect1_made)
                    last_group = last_round and b == RING - 1
                    if last_group:
                        add_windows(group - 1, (b - 1) % 2, D, summed1, added1, False)
                    dve.wait_ge(hg_landed[b], 16 * G * (r + 1))
                    dve.wait_ge(emb_made, group + 1)
                    if not (first and b < 2):
                        dve.wait_ge(relu_made, group - 1)
                    nc.vector.tensor_tensor(prod[b % 2][:, :, :],
                                            ps_edge[b % 2][:, 0:G * D].rearrange("p (j c) -> p j c", c=D),
                                            kv[b][:, :, 0:D], ALU.add).then_inc(message_made, 1)
                    if not (first and b == 0 or last_group):
                        add_windows(group - 1, (b - 1) % 2, D, summed1, added1, first and b == 1)

            rounds(dve, edges1)
            add_windows(GROUPS - 1, (RING - 1) % 2, D, summed1, added1, False)

            for half in range(2):
                for k, (ts,) in jobs_of("z1", half, "V"):
                    bank = filled("z1", k)
                    nc.vector.tensor_scalar(mT[:, ts.start * NP:ts.stop * NP], bank[0:D, 0:len(ts) * NP],
                                            cols_sb[:, 4:5], 0.0, ALU.add, ALU.max).then_inc(emptied_dve, 1)
            dve.wait_ge(b2_added, 1)
            for half in range(2):
                add_banks("out", HALVES[half], h_sb, x_sb)


WEIGHT_DMAS = 10


def kernel(**inputs):
    import numpy as _np
    import concourse.bacc as _bacc
    from concourse import mybir as _mybir
    from concourse.bass_utils import run_bass_kernel_spmd as _run

    a = {k: _np.asarray(v) for k, v in inputs.items()}
    edges = TILES * P

    def padded(v, fill):
        return _np.concatenate([v, _np.full((edges - E,) + v.shape[1:], fill, v.dtype)])

    src, dst = padded(a["src"], 0), padded(a["dst"], -1)
    edge_attr = padded(a["edge_attr_32"], 0)
    wqkv = _np.concatenate([a["L0_gnn_w_q"], a["L0_gnn_w_k"], a["L0_gnn_w_v"]], axis=1)
    laid = {
        "x": a["x"],
        "srcg": src.reshape(GROUPS, G, P).transpose(0, 2, 1),
        "dstT": dst.reshape(TILES, P).T,
        "dstrow": dst.reshape(GROUPS, G, P),
        "eaT": _np.concatenate([edge_attr.reshape(GROUPS, G, P, EC).transpose(0, 3, 1, 2),
                                _np.ones((GROUPS, 1, G, P), edge_attr.dtype)], axis=1),
        "wqkv": wqkv,
        "wo": a["L0_gnn_w_o"],
        "ff1w": a["L0_gnn_ff1_w"], "ff1b": a["L0_gnn_ff1_b"].reshape(2, P).T, "ff2w": a["L0_gnn_ff2_w"],
        "weT": _np.concatenate([a["L1_gnn_We"].T, a["L1_gnn_be"][None]]),
        "w1T": a["L1_gnn_W1"].T, "w2T": a["L1_gnn_W2"].T,
        "cols": _np.stack([a["L0_gnn_ln1_g"], a["L0_gnn_ln1_b"], a["L0_gnn_ln2_g"], a["L0_gnn_ln2_b"],
                           a["L1_gnn_b1"]], axis=1),
        "rows": _np.stack([a["L0_gnn_ff2_b"], a["L1_gnn_b2"]])[None],
    }
    nc = _bacc.Bacc("TRN2", target_bir_lowering=False, num_devices=1)
    arrays, args = {}, []
    for name, v in laid.items():
        v = _np.ascontiguousarray(v)
        arrays[f"in_{name}"] = v
        args.append(nc.dram_tensor(f"in_{name}", v.shape, _mybir.dt.from_np(v.dtype), kind="ExternalInput").ap())
    f32 = _mybir.dt.float32
    tables = [nc.dram_tensor("q_table", (ACC_COLS, D), f32, kind="Internal").ap(),
              nc.dram_tensor("kv_table", (N, 2 * D), f32, kind="Internal").ap(),
              nc.dram_tensor("h_table", (N, D), f32, kind="Internal").ap(),
              nc.dram_tensor("rel_table", (GROUPS, G * P), _mybir.dt.bfloat16, kind="Internal").ap()]
    out = nc.dram_tensor("out_0", (N, D), f32, kind="ExternalOutput").ap()
    build(nc, *args, *tables, out)
    r = _run(nc, [arrays], core_ids=[0])
    return r.results[0]["out_0"]
```
